# Optimizing a Trainium2 kernel written in Bass

```python
import numpy as np
import jax
import jax.numpy as jnp

def _softmax(x, axis=-1):
    return jax.nn.softmax(x, axis=axis)

def _gelu(x):
    return jax.nn.gelu(x, approximate=True)

def _silu(x):
    return jax.nn.silu(x)

def _sigmoid(x):
    return jax.nn.sigmoid(x)

def _layernorm(x, axis=-1, eps=1e-05):
    m = jnp.mean(x, axis=axis, keepdims=True)
    v = jnp.var(x, axis=axis, keepdims=True)
    return (x - m) / jnp.sqrt(v + eps)

def _scatter_add(tgt, idx, src, axis=0):
    return tgt.at[idx].add(src)

def _segment_sum(src, seg, n):
    return jax.ops.segment_sum(src, seg, n)
kernel_name = 'mk_seq_postln_d1_jaxref_r8_32909e'

def setup_inputs(seed: int=0):
    np.random.seed(seed)
    _w = jnp.asarray

    def _L0_attn_setup():
        import jax, jax.numpy as jnp
        import numpy as np
        B, T, D_MODEL = (4, 256, 256)
        NUM_HEADS, HEAD_SIZE = (16, 128)
        MODEL_SIZE = 256
        key = jax.random.key(seed)
        ks = jax.random.split(key, 9)
        s = 0.02 / np.sqrt(D_MODEL)
        so = 0.02 / np.sqrt(NUM_HEADS * HEAD_SIZE)
        return {'query': jax.random.normal(ks[0], (B, T, D_MODEL), jnp.float32), 'w_q': jax.random.normal(ks[1], (D_MODEL, NUM_HEADS * HEAD_SIZE), jnp.float32) * s, 'b_q': jnp.zeros((NUM_HEADS * HEAD_SIZE,), jnp.float32), 'w_k': jax.random.normal(ks[2], (D_MODEL, NUM_HEADS * HEAD_SIZE), jnp.float32) * s, 'b_k': jnp.zeros((NUM_HEADS * HEAD_SIZE,), jnp.float32), 'w_v': jax.random.normal(ks[3], (D_MODEL, NUM_HEADS * HEAD_SIZE), jnp.float32) * s, 'b_v': jnp.zeros((NUM_HEADS * HEAD_SIZE,), jnp.float32), 'w_o': jax.random.normal(ks[4], (NUM_HEADS * HEAD_SIZE, MODEL_SIZE), jnp.float32) * so, 'b_o': jnp.zeros((MODEL_SIZE,), jnp.float32)}
    _L0_attn_in = _L0_attn_setup()

    def _L0_ffn_setup():
        import jax, jax.numpy as jnp
        import numpy as np
        E = 8
        TOP_K = 2
        D = 256
        DE = 176
        DS = 352
        B, S = (2, 256)
        key = jax.random.key(seed)
        ks = jax.random.split(key, 8)
        std = 0.02
        return {'x': jax.random.normal(ks[0], (B, S, D), jnp.float32), 'W_router': jax.random.normal(ks[1], (D, E), jnp.float32) * std, 'We_gate': jax.random.normal(ks[2], (E, D, DE), jnp.float32) * std, 'We_up': jax.random.normal(ks[3], (E, D, DE), jnp.float32) * std, 'We_down': jax.random.normal(ks[4], (E, DE, D), jnp.float32) * std, 'Ws_gate': jax.random.normal(ks[5], (D, DS), jnp.float32) * std, 'Ws_up': jax.random.normal(ks[6], (D, DS), jnp.float32) * std, 'Ws_down': jax.random.normal(ks[7], (DS, D), jnp.float32) * std}
    _L0_ffn_in = _L0_ffn_setup()
    _d = {'L0_attn_query': _L0_attn_in['query'], 'L0_attn_w_q': _L0_attn_in['w_q'], 'L0_attn_b_q': _L0_attn_in['b_q'], 'L0_attn_w_k': _L0_attn_in['w_k'], 'L0_attn_b_k': _L0_attn_in['b_k'], 'L0_attn_w_v': _L0_attn_in['w_v'], 'L0_attn_b_v': _L0_attn_in['b_v'], 'L0_attn_w_o': _L0_attn_in['w_o'], 'L0_attn_b_o': _L0_attn_in['b_o'], 'L0_ffn_W_router': _L0_ffn_in['W_router'], 'L0_ffn_We_gate': _L0_ffn_in['We_gate'], 'L0_ffn_We_up': _L0_ffn_in['We_up'], 'L0_ffn_We_down': _L0_ffn_in['We_down'], 'L0_ffn_Ws_gate': _L0_ffn_in['Ws_gate'], 'L0_ffn_Ws_up': _L0_ffn_in['Ws_up'], 'L0_ffn_Ws_down': _L0_ffn_in['Ws_down']}
    _x0 = _d['L0_attn_query']
    _d['L0_attn_query'] = jax.random.normal(jax.random.fold_in(jax.random.key(seed), 1), (4, 1024, 256), dtype=_x0.dtype)
    del _x0
    return _d

def reference(L0_attn_query, L0_attn_w_q, L0_attn_b_q, L0_attn_w_k, L0_attn_b_k, L0_attn_w_v, L0_attn_b_v, L0_attn_w_o, L0_attn_b_o, L0_ffn_W_router, L0_ffn_We_gate, L0_ffn_We_up, L0_ffn_We_down, L0_ffn_Ws_gate, L0_ffn_Ws_up, L0_ffn_Ws_down):

    def _L0_attn_ref(query, w_q, b_q, w_k, b_k, w_v, b_v, w_o, b_o):
        import jax, jax.numpy as jnp
        import numpy as np
        B, T, D_MODEL = (4, 256, 256)
        NUM_HEADS, HEAD_SIZE = (16, 128)
        MODEL_SIZE = 256
        B_, T_, _ = query.shape
        q = (query @ w_q + b_q).reshape(B_, T_, NUM_HEADS, HEAD_SIZE)
        k = (query @ w_k + b_k).reshape(B_, T_, NUM_HEADS, HEAD_SIZE)
        v = (query @ w_v + b_v).reshape(B_, T_, NUM_HEADS, HEAD_SIZE)
        logits = jnp.einsum('bthd,bThd->bhtT', q, k) * jax.lax.rsqrt(jnp.float32(HEAD_SIZE))
        i = jnp.arange(T_, dtype=jnp.int32)[:, None]
        j = jnp.arange(T_, dtype=jnp.int32)
        mask = (i >= j).astype(logits.dtype)
        logits = logits - 10000000000.0 * (1.0 - mask)
        weights = jax.nn.softmax(logits, axis=-1)
        attn = jnp.einsum('bhtT,bThd->bthd', weights, v).reshape(B_, T_, NUM_HEADS * HEAD_SIZE)
        out = attn @ w_o + b_o
        return out

    def _L0_ffn_ref(x, W_router, We_gate, We_up, We_down, Ws_gate, Ws_up, Ws_down):
        import jax, jax.numpy as jnp
        import numpy as np
        E = 8
        TOP_K = 2
        D = 256
        DE = 176
        DS = 352
        B, S = (2, 256)
        b, s, d = x.shape
        shared = jax.nn.silu(x @ Ws_gate) * (x @ Ws_up) @ Ws_down
        scores = jax.nn.softmax(x @ W_router, axis=-1)
        topk_vals, topk_idx = jax.lax.top_k(scores, TOP_K)
        onehot = jax.nn.one_hot(topk_idx, E, dtype=x.dtype)
        combine = jnp.einsum('bsk,bske->bse', topk_vals, onehot)
        combine = combine.reshape(b * s, E)
        xf = x.reshape(b * s, d)
        h = jax.nn.silu(jnp.einsum('td,edh->eth', xf, We_gate)) * jnp.einsum('td,edh->eth', xf, We_up)
        y_all = jnp.einsum('eth,ehd->etd', h, We_down)
        routed = jnp.einsum('etd,te->td', y_all, combine)
        return routed.reshape(b, s, d) + shared
    x = L0_attn_query
    x = _layernorm(x + _L0_attn_ref(x, L0_attn_w_q, L0_attn_b_q, L0_attn_w_k, L0_attn_b_k, L0_attn_w_v, L0_attn_b_v, L0_attn_w_o, L0_attn_b_o), axis=-1)
    x = _layernorm(x + _L0_ffn_ref(x, L0_ffn_W_router, L0_ffn_We_gate, L0_ffn_We_up, L0_ffn_We_down, L0_ffn_Ws_gate, L0_ffn_Ws_up, L0_ffn_Ws_down), axis=-1)
    return x

_drawn_inputs = setup_inputs


def setup_inputs(seed=0):
    import zlib

    import numpy as np

    out = dict(_drawn_inputs(seed))
    spreads = {'L0_attn_b_q': (0.0, 2.0),
     'L0_attn_b_k': (0.0, 2.0),
     'L0_attn_b_v': (0.0, 0.8),
     'L0_attn_b_o': (0.0, 0.1)}
    factors = {'L0_attn_w_q': 64.0,
     'L0_attn_w_k': 64.0,
     'L0_attn_w_v': 8.0,
     'L0_attn_w_o': 8.0,
     'L0_ffn_W_router': 8.0,
     'L0_ffn_We_gate': 8.0,
     'L0_ffn_We_up': 8.0,
     'L0_ffn_We_down': 8.0,
     'L0_ffn_Ws_gate': 2.89,
     'L0_ffn_Ws_up': 2.865,
     'L0_ffn_Ws_down': 2.86}
    for name, (base, spread) in spreads.items():
        noise = np.random.default_rng([zlib.crc32(name.encode()), seed]).standard_normal(out[name].shape)
        drawn = base * np.exp(spread * noise) if base else spread * noise
        out[name] = jnp.asarray(drawn.astype(out[name].dtype))
    for name, factor in factors.items():
        out[name] = (out[name] * factor).astype(out[name].dtype)
    return out
```

```python
from contextlib import ExitStack

import concourse.bass as bass
from concourse import mybir

F32 = mybir.dt.float32
F32R = mybir.dt.float32r
ALU = mybir.AluOpType
ACT = mybir.ActivationFunctionType
AX = mybir.AxisListType

P = 128
BANK = 512


def wait_alone(engine, passed, signal, count):
    engine.wait_ge(signal, count)
    engine.sem_inc(passed, 1)


def attention_schedule():
    count = {"slot": 0, "proj": 0, "row": 0, "turn": 0, "unit": 0, "out": 0}
    steps, frees = [], []

    def take(kind):
        count[kind] += 1
        return count[kind] - 1

    def project(what, head=0):
        steps.append(dict(kind=what, head=head, slot=take("slot"), proj=take("proj")))
        frees.append("proj_low_done")

    def scores(head, quad, i):
        steps.append(dict(kind="score", head=head, quad=quad, i=i, slot=take("slot"), row=take("row")))
        frees.append("exp_done")

    def output(j):
        steps.append(dict(kind="output", j=j, slot=take("slot"), out=take("out")))
        frees.append("output_added")

    def unit_steps(head, quad, rows):
        unit, n = take("unit"), 4 * quad + 4
        base = count["turn"]
        count["turn"] += n
        turn = lambda kb: dict(kind="turn", quad=quad, kb=kb, turn=base + kb, rows=rows)
        listed = [[turn(0), turn(1)]]
        for kb in range(n):
            pair = [dict(kind="pv", head=head, quad=quad, kb=kb, turn=base + kb, unit=unit, last=kb == n - 1)]
            if kb + 2 < n:
                pair.append(turn(kb + 2))
            listed.append(pair)
        listed[-1].append(dict(kind="unit_end", head=head, quad=quad, unit=unit, turn=base + n - 1))
        return listed

    def block(head, quad, old_head, old_quad, rows):
        lots = unit_steps(old_head, old_quad, rows)
        pairs = lots[1:]
        a, b = (len(pairs) * 3 + 7) // 8, (len(pairs) * 3 + 3) // 4
        scores(head, quad, 0)
        scores(head, quad, 1)
        steps.extend(lots[0])
        for i, some in ((2, pairs[:a]), (3, pairs[a:b]), (None, pairs[b:])):
            for pair in some:
                steps.extend(pair)
            if i is not None:
                scores(head, quad, i)

    project("q", 0)
    project("k", 0)
    block(0, 0, 1, 1, 0)
    project("v", 0)
    project("v", 1)
    output(0)
    output(1)
    block(0, 1, 0, 0, 4)
    project("q", 1)
    project("k", 1)
    block(1, 0, 0, 1, 8)
    block(1, 1, 1, 0, 12)
    return steps, count, frees


def layer(nc, query, w_q, b_q, w_k, b_k, w_v, b_v, w_o, b_o, w_router, we_gate, we_up, we_down,
          ws_gate, ws_up, ws_down, out):
    B, T, D = query.shape
    HD = P
    H = w_q.shape[1] // HD
    PAIRS = H // 2
    DC = D // P
    TB = T // P
    NB = B * TB
    E, _, DE = we_gate.shape
    DS = ws_gate.shape[1]
    ROUTED = E * DE
    RC = ROUTED // P
    FT = ROUTED + DS
    CHUNKS = [(c * P, min(P, FT - c * P)) for c in range((FT + P - 1) // P)]
    NCH = len(CHUNKS)
    TILE = 4 * P
    TILES = B * T // TILE
    assert (D, TB, HD) == (2 * P, 8, P) and ROUTED == RC * P and H % 2 == 0
    SCALE = float(HD) ** -0.5
    MASKED = -1e10 / SCALE
    EPS = 1e-5

    STEPS, COUNT, FREES = attention_schedule()
    SLOTS, ROWS, TURNS, UNITS, PROJ, OUTS = (COUNT[k] for k in ("slot", "row", "turn", "unit", "proj", "out"))
    LAST_UNIT = [s for s in STEPS if s.get("unit") == 0 or (s["kind"] == "turn" and s["turn"] < TB)]
    TAIL = LAST_UNIT + [dict(s, slot=s["j"]) for s in STEPS if s["kind"] == "output"]

    ctx = ExitStack()
    with ctx:
        def sem(name):
            return ctx.enter_context(nc.semaphore(name))

        totals = {}

        def counted(name, total):
            s = sem(name)
            totals[name] = (s, total)
            return s

        slot_full = counted("slot_full", SLOTS)
        turned = counted("turned", TURNS)
        pv_done = counted("pv_done", TURNS)
        exp_done = counted("exp_done", ROWS)
        turn_high = counted("turn_high", TURNS)
        unit_high = counted("unit_high", UNITS)
        proj_high = counted("proj_high", PROJ)
        part_max = counted("part_max", ROWS)
        shift_ready = counted("shift_ready", ROWS)
        inverse_ready = counted("inverse_ready", ROWS)
        turn_low_done = counted("turn_low_done", TURNS)
        unit_low_done = counted("unit_low_done", UNITS)
        proj_low_done = counted("proj_low_done", PROJ)
        output_added = counted("output_added", OUTS)
        divided = counted("divided", ROWS)
        w_high = counted("w_high", 4)
        wv_ready = counted("wv_ready", 1)
        wqk_ready = [counted(f"wqk{h}_ready", 1) for h in range(2)]
        wo_ready = counted("wo_ready", 1)
        raw_qk = [sem(f"raw_qk{h}") for h in range(2)]
        raw_v = sem("raw_v")
        raw_o = sem("raw_o")
        xt_full = counted("xt_full", DC)
        xt_high = counted("xt_high", DC)
        xt_low_done = counted("xt_low_done", DC)
        x_staged = sem("x_staged")
        consts_in = sem("consts_in")
        bias_in = sem("bias_in")
        bias_turned = sem("bias_turned")
        stream_in = sem("stream_in")
        passed = sem("passed")
        ident_zero = sem("ident_zero")
        ident_ready = sem("ident_ready")
        free_event = {"proj_low_done": proj_low_done, "exp_done": exp_done, "output_added": output_added}

        def at(name, n, i):
            return n * totals[name][1] + totals[name][1] + i

        def slot_use_before(k):
            j = (k - 2) % SLOTS
            name = FREES[j]
            done = FREES[:j + 1].count(name)
            return name, done - (FREES.count(name) if k < 2 else 0)

        def sb(stack, name, shape, dt=F32):
            return stack.enter_context(nc.sbuf_tensor(name, shape, dt))

        stream = sb(ctx, "stream", [P, (B + 1) * TB, D])
        ident = sb(ctx, "ident", [P, P])
        bo_rows = sb(ctx, "bo_rows", [P, D])

        with ExitStack() as st:
            maskneg = sb(st, "maskneg", [P, P])
            bias_cols = sb(st, "bias_cols", [P, 3, H])
            bias_rows = sb(st, "bias_rows", [3 * H, HD])
            x_stage = sb(st, "x_stage", [P, TB, D])
            xT = [sb(st, f"xT_{p}", [P, DC, T], F32R) for p in ("high", "low")]
            raw_wqk = [sb(st, f"raw_wqk{h}", [P, 2, DC, HD]) for h in range(2)]
            raw_wv = sb(st, "raw_wv", [P, DC, 2 * HD])
            raw_wo = sb(st, "raw_wo", [P, 2, D])
            wqk = [[sb(st, f"wqk{h}_{p}", [P, 2, DC, HD], F32R) for p in ("high", "low")] for h in range(2)]
            wv = [sb(st, f"wv_{p}", [P, DC, 2 * HD], F32R) for p in ("high", "low")]
            wo = [sb(st, f"wo_{p}", [P, 2, D], F32R) for p in ("high", "low")]
            qT = [[sb(st, f"qT{h}_{p}", [P, T], F32R) for p in ("high", "low")] for h in range(2)]
            kT = [[sb(st, f"kT{h}_{p}", [P, T], F32R) for p in ("high", "low")] for h in range(2)]
            v = [sb(st, f"v_{p}", [P, TB, 2 * HD], F32R) for p in ("high", "low")]
            probs = [sb(st, f"probs{g}", [P, 4, 4 * (g + 1) * P]) for g in range(2)]
            probsT = [[sb(st, f"probsT{i}_{p}", [P, 4 * P], F32R) for p in ("high", "low")] for i in range(2)]
            headT = [sb(st, f"headT_{p}", [P, 2, T], F32R) for p in ("high", "low")]
            row_max = sb(st, "row_max", [P, 2, ROWS])
            shift = sb(st, "shift", [P, ROWS])
            row_sum = sb(st, "row_sum", [P, ROWS])
            inverse = sb(st, "inverse", [P, ROWS])

            slots = [st.enter_context(nc.psum_tensor(f"slot{i}", [P, 2 * BANK], F32)) for i in range(2)]
            turnP = [st.enter_context(nc.psum_tensor(f"turnP{i}", [P, BANK], F32)) for i in range(2)]
            unitP = [st.enter_context(nc.psum_tensor(f"unitP{i}", [P, BANK], F32)) for i in range(2)]

            with nc.Block() as block:
                @block.sync
                def _(sp):
                    for m, bias in enumerate((b_q, b_k, b_v)):
                        sp.dma_start(bias_rows[m * H:(m + 1) * H, :], bias.rearrange("(h d) -> h d", d=HD)).then_inc(bias_in, 16)

                @block.tensor
                def _(pe):
                    pe.wait_ge(bias_in, 3 * 16)
                    pe.wait_ge(ident_ready, 1)
                    pe.transpose(turnP[0][:, 0:3 * H], bias_rows[:], ident[0:3 * H, 0:3 * H]).then_inc(bias_turned, 1)

                @block.scalar
                def _(act):
                    act.wait_ge(bias_turned, 1)
                    act.activation(bias_cols[:].rearrange("p m h -> p (m h)"), turnP[0][:, 0:3 * H], ACT.Copy)

                @block.gpsimd
                def _(pool):
                    pool.memset(ident[:], 0.0).then_inc(ident_zero, 1)
                    pool.memset(maskneg[:], 0.0).then_inc(ident_zero, 1)
                    pool.wait_ge(ident_zero, 2)
                    pool.affine_select(out=ident[:], in_=ident[:], compare_op=ALU.not_equal, fill=1.0, base=0,
                                       pattern=[[-1, P]], channel_multiplier=1).then_inc(ident_ready, 1)
                    pool.affine_select(out=maskneg[:], in_=maskneg[:], compare_op=ALU.is_ge, fill=MASKED, base=0,
                                       pattern=[[-1, P]], channel_multiplier=1).then_inc(ident_ready, 1)
                    for part in range(2):
                        pool.memset(wo[part][:].bitcast(F32), 0.0)
                        pool.memset(v[part][:].bitcast(F32), 0.0)
                    pool.wait_ge(ident_ready, 2)
                    for s, total in totals.values():
                        pool.sem_inc(s, total)

                @block.vector
                def _(dve):
                    for g in range(2):
                        dve.memset(probs[g][:], 0.0)
                    for part in range(2):
                        dve.memset(headT[part][:].bitcast(F32), 0.0)
                    dve.memset(stream[:, 0:TB, :], 0.0)

            with nc.Block() as block:
                @block.sync
                def _(sp):
                    w_of = {"q": w_q, "k": w_k}

                    def load_qk(head, pair):
                        for m, w in enumerate((w_q, w_k)):
                            sp.dma_start(raw_wqk[head][:, m],
                                         w.rearrange("(c p) n -> p c n", p=P)[:, :, bass.ds(pair * 2 * HD + head * HD, HD)]
                                         ).then_inc(raw_qk[head], 16)

                    def load_x(b):
                        sp.dma_start(x_stage[:], query[bass.ds(b, 1)].rearrange("o (t p) d -> p (o t) d", p=P)
                                     ).then_inc(x_staged, 16)

                    load_x(0)
                    sp.dma_start(bo_rows[:], b_o.rearrange("(o d) -> o d", o=1).to_broadcast([P, D])).then_inc(consts_in, 16)

                    def loads(n, pair):
                        sp.wait_ge(wqk_ready[0], at("wqk0_ready", n, 0))
                        load_qk(0, pair)
                        sp.wait_ge(wqk_ready[1], at("wqk1_ready", n, 0))
                        load_qk(1, pair)
                        sp.wait_ge(wv_ready, at("wv_ready", n, 0))
                        sp.dma_start(raw_wv[:], w_v.rearrange("(c p) n -> p c n", p=P)[:, :, bass.ds(pair * 2 * HD, 2 * HD)]
                                     ).then_inc(raw_v, 16)
                        sp.wait_ge(wo_ready, at("wo_ready", n, 0))
                        sp.dma_start(raw_wo[:], w_o.rearrange("(g h d) n -> d (g h) n", h=2, d=HD)[:, bass.ds(pair * 2, 2), :]
                                     ).then_inc(raw_o, 16)

                    with sp.Fori(0, B) as b:
                        loads(b * PAIRS, 0)
                        sp.dma_start(stream[:, bass.ds((b + 1) * TB, TB), :],
                                     query[bass.ds(b, 1)].rearrange("o (t p) d -> p (o t) d", p=P)).then_inc(stream_in, 16)
                        with sp.Fori(1, PAIRS) as g:
                            loads(b * PAIRS + g, g)
                        sp.wait_ge(xt_full, at("xt_full", b, DC))
                        load_x((b + 1) % B)
                    sp.wait_ge(wqk_ready[0], at("wqk0_ready", B * PAIRS, 0))
                    load_qk(0, 0)
                    sp.wait_ge(raw_qk[0], 2 * 16 * (B * PAIRS + 1))
                    sp.wait_ge(x_staged, 16 * (B + 1))

                @block.tensor
                def _(pe):
                    def three(dst, a, b, ra, rb, first, last):
                        for j, (x, y) in enumerate(((1, 0), (0, 0), (0, 1))):
                            made = pe.matmul(dst, a[x][ra], b[y][rb], start=first and j == 0, stop=last and j == 2)
                        return made

                    def wait_slot(n, k):
                        name, i = slot_use_before(k)
                        pe.wait_ge(free_event[name], at(name, n, i))

                    def turn_x(b):
                        for c in range(DC):
                            if c == 0:
                                pe.wait_ge(x_staged, b * 16 + 16)
                            name, i = slot_use_before(c)
                            pe.wait_ge(free_event[name], at(name, b * PAIRS, i))
                            for t in range(TB):
                                made = pe.transpose(slots[c][:, t * P:(t + 1) * P],
                                                    x_stage[:, t, c * P:(c + 1) * P], ident[:])
                            made.then_inc(xt_full, 1)

                    def run(n, steps, b=None):
                        for s in steps:
                            kind = s["kind"]
                            slot = slots[s["slot"] % 2] if "slot" in s else None
                            if kind in "qk":
                                h = s["head"]
                                if s["slot"] < 2 and b is not None:
                                    if s["slot"] == 0:
                                        pe.wait_ge(xt_low_done, at("xt_low_done", b, DC))
                                else:
                                    wait_slot(n, s["slot"])
                                if kind == "q":
                                    pe.wait_ge(wqk_ready[h], at(f"wqk{h}_ready", n, 1))
                                m = "qk".index(kind)
                                for half in range(2):
                                    for c in range(DC):
                                        made = three(slot[:, half * BANK:(half + 1) * BANK], wqk[h], xT,
                                                     (slice(None), m, c), (slice(None), c, slice(half * BANK, (half + 1) * BANK)),
                                                     c == 0, c == DC - 1)
                                made.then_inc(slot_full, 1)
                            elif kind == "v":
                                wait_slot(n, s["slot"])
                                if s["head"] == 0:
                                    pe.wait_ge(wv_ready, at("wv_ready", n, 1))
                                for t in range(4):
                                    tb = 4 * s["head"] + t
                                    for c in range(DC):
                                        made = three(slot[:, t * 2 * HD:(t + 1) * 2 * HD], xT, wv,
                                                     (slice(None), c, slice(tb * P, (tb + 1) * P)), (slice(None), c),
                                                     c == 0, c == DC - 1)
                                made.then_inc(slot_full, 1)
                            elif kind == "output":
                                wait_slot(n, s["slot"])
                                if s["j"] == 0:
                                    pe.wait_ge(wo_ready, at("wo_ready", n, 0))
                                    pe.wait_ge(unit_low_done, at("unit_low_done", n, 1))
                                for t in range(4):
                                    tb = 4 * s["j"] + t
                                    for h in range(2):
                                        made = three(slot[:, t * D:(t + 1) * D], headT, wo,
                                                     (slice(None), h, slice(tb * P, (tb + 1) * P)), (slice(None), h),
                                                     h == 0, h == 1)
                                made.then_inc(slot_full, 1)
                            elif kind == "score":
                                h, qi = s["head"], 4 * s["quad"] + s["i"]
                                wait_slot(n, s["slot"])
                                if s["quad"] == 0 and s["i"] == 0:
                                    pe.wait_ge(proj_low_done, at("proj_low_done", n, (2, PROJ)[h]))
                                keys = (qi + 1) * P
                                spans = [(0, min(BANK, max(keys, 2 * P)))]
                                if keys > BANK:
                                    spans.append((BANK, BANK + max(keys - BANK, 2 * P)))
                                for j, (x, y) in enumerate(((0, 0), (0, 1), (1, 0))):
                                    for lo, hi in spans:
                                        made = pe.matmul(slot[:, lo:hi], qT[h][x][:, qi * P:(qi + 1) * P],
                                                         kT[h][y][:, lo:hi], start=j == 0, stop=j == 2)
                                made.then_inc(slot_full, 1)
                            elif kind == "turn":
                                g, kb = s["quad"], s["kb"]
                                if kb == 0:
                                    pe.wait_ge(divided, at("divided", n, s["rows"]))
                                lo = min(max(kb - 4 * g, 0), 2)
                                for i in range(lo, 4):
                                    made = pe.transpose(turnP[s["turn"] % 2][:, i * P:(i + 1) * P],
                                                        probs[g][:, i, kb * P:(kb + 1) * P], ident[:])
                                made.then_inc(turned, 1)
                            elif kind == "pv":
                                g, kb, h = s["quad"], s["kb"], s["head"]
                                if kb == 0:
                                    pe.wait_ge(unit_low_done, at("unit_low_done", n, s["unit"] - 1))
                                    if s["unit"] == 1:
                                        pe.wait_ge(proj_low_done, at("proj_low_done", n, 4))
                                pe.wait_ge(turn_low_done, at("turn_low_done", n, s["turn"] + 1))
                                lo = min(max(kb - 4 * g, 0), 2) * P
                                pt = probsT[s["turn"] % 2]
                                made = three(unitP[s["unit"] % 2][:, lo:], v, pt,
                                             (slice(None), kb, slice(h * HD, (h + 1) * HD)), (slice(None), slice(lo, 4 * P)),
                                             kb == 0, s["last"])
                                made.then_inc(pv_done, 1)

                    with pe.Fori(0, B) as b:
                        turn_x(b)
                        run(b * PAIRS, STEPS, b)
                        with pe.Fori(1, PAIRS) as g:
                            run(b * PAIRS + g, STEPS)
                    run(B * PAIRS, TAIL)

                @block.scalar
                def _(act):
                    def run(n, steps, g):
                        for s in steps:
                            kind = s["kind"]
                            slot = slots[s["slot"] % 2] if "slot" in s else None
                            if kind in "qk":
                                dst = (qT if kind == "q" else kT)[s["head"]][0]
                                wait_alone(act, passed, slot_full, at("slot_full", n, s["slot"] + 1))
                                act.activation(dst[:], slot[:], ACT.Identity,
                                               bias=bias_cols[:, "qk".index(kind), bass.ds(g * 2 + s["head"], 1)]
                                               ).then_inc(proj_high, 1)
                            elif kind == "v":
                                act.wait_ge(slot_full, at("slot_full", n, s["slot"] + 1))
                                act.activation(v[0][:, 4 * s["head"]:4 * s["head"] + 4, :],
                                               slot[:].rearrange("p (t n) -> p t n", t=4), ACT.Copy).then_inc(proj_high, 1)
                            elif kind == "score":
                                quad, i, row = s["quad"], s["i"], s["row"]
                                keys = (4 * quad + i + 1) * P
                                act.wait_ge(shift_ready, at("shift_ready", n, row + 1))
                                act.activation(probs[quad][:, i, 0:keys], slot[:, 0:keys], ACT.Exp,
                                               bias=shift[:, row:row + 1], scale=SCALE,
                                               accum_out=row_sum[:, row:row + 1]).then_inc(exp_done, 1)
                            elif kind == "turn":
                                lo = min(max(s["kb"] - 4 * s["quad"], 0), 2) * P
                                act.wait_ge(turned, at("turned", n, s["turn"] + 1))
                                act.activation(probsT[s["turn"] % 2][0][:, lo:], turnP[s["turn"] % 2][:, lo:],
                                               ACT.Copy).then_inc(turn_high, 1)
                            elif kind == "unit_end":
                                h, quad = s["head"], s["quad"]
                                head = (g * 2 - 1) if s["unit"] == 0 else (g * 2 + h)
                                if s["unit"] == 0 and isinstance(g, int) and g == 0:
                                    head = H - 1
                                wait_alone(act, passed, pv_done, at("pv_done", n, s["turn"] + 1))
                                act.activation(headT[0][:, h, quad * BANK:(quad + 1) * BANK], unitP[s["unit"] % 2][:],
                                               ACT.Identity, bias=bias_cols[:, 2, bass.ds(head, 1)]).then_inc(unit_high, 1)

                    act.wait_ge(consts_in, 16)
                    with act.Fori(0, B) as b:
                        for c in range(DC):
                            act.wait_ge(xt_full, at("xt_full", b, c + 1))
                            act.activation(xT[0][:, c, :], slots[c][:], ACT.Copy).then_inc(xt_high, 1)
                        run(b * PAIRS, STEPS, 0)
                        with act.Fori(1, PAIRS) as g:
                            run(b * PAIRS + g, STEPS, g)
                    run(B * PAIRS, TAIL, 0)

                @block.vector
                def _(dve):
                    def run(n, steps, g, out_batch):
                        waiting = []

                        def invert():
                            for row in waiting:
                                dve.wait_ge(exp_done, at("exp_done", n, row + 1))
                                dve.reciprocal(inverse[:, row:row + 1], row_sum[:, row:row + 1]).then_inc(inverse_ready, 1)
                            waiting.clear()

                        for s in steps:
                            kind = s["kind"]
                            slot = slots[s["slot"] % 2] if "slot" in s else None
                            if kind in "qk":
                                parts = (qT if kind == "q" else kT)[s["head"]]
                                dve.wait_ge(proj_high, at("proj_high", n, s["proj"] + 1))
                                dve.scalar_tensor_tensor(parts[1][:], slot[:],
                                                         bias_cols[:, "qk".index(kind), bass.ds(g * 2 + s["head"], 1)],
                                                         parts[0][:].bitcast(F32), ALU.add, ALU.subtract).then_inc(proj_low_done, 1)
                                invert()
                            elif kind == "v":
                                r = slice(4 * s["head"], 4 * s["head"] + 4)
                                dve.wait_ge(proj_high, at("proj_high", n, s["proj"] + 1))
                                dve.tensor_tensor(v[1][:, r, :], slot[:].rearrange("p (t n) -> p t n", t=4),
                                                  v[0][:, r, :].bitcast(F32), ALU.subtract).then_inc(proj_low_done, 1)
                                invert()
                            elif kind == "output":
                                dst = stream[:, bass.ds(out_batch * TB + 4 * s["j"], 4), :]
                                dve.wait_ge(slot_full, at("slot_full", n, s["slot"] + 1))
                                dve.tensor_tensor(dst, slot[:].rearrange("p (t n) -> p t n", t=4), dst,
                                                  ALU.add).then_inc(output_added, 1)
                                invert()
                            elif kind == "score":
                                qi, row = 4 * s["quad"] + s["i"], s["row"]
                                diagonal = slot[:, qi * P:(qi + 1) * P]
                                wait_alone(dve, passed, slot_full, at("slot_full", n, s["slot"] + 1))
                                made = dve.tensor_tensor_reduce(diagonal, diagonal, maskneg[:], 1.0, -3e38, ALU.add, ALU.max,
                                                                row_max[:, 0, row:row + 1])
                                if qi:
                                    made = dve.reduce_max(row_max[:, 1, row:row + 1], slot[:, 0:qi * P], AX.X)
                                made.then_inc(part_max, 1)
                                invert()
                                dve.wait_ge(part_max, at("part_max", n, row + 1))
                                dve.tensor_scalar(shift[:, row:row + 1], row_max[:, 0, row:row + 1],
                                                  row_max[:, 1, row:row + 1] if qi else -3e38, -SCALE,
                                                  ALU.max, ALU.mult).then_inc(shift_ready, 1)
                                waiting.append(row)
                            elif kind == "turn":
                                lo = min(max(s["kb"] - 4 * s["quad"], 0), 2) * P
                                pt = probsT[s["turn"] % 2]
                                dve.wait_ge(turn_high, at("turn_high", n, s["turn"] + 1))
                                dve.tensor_tensor(pt[1][:, lo:], turnP[s["turn"] % 2][:, lo:], pt[0][:, lo:].bitcast(F32),
                                                  ALU.subtract).then_inc(turn_low_done, 1)
                                invert()
                            elif kind == "unit_end":
                                h, quad = s["head"], s["quad"]
                                head = (g * 2 - 1) if s["unit"] == 0 else (g * 2 + h)
                                if s["unit"] == 0 and isinstance(g, int) and g == 0:
                                    head = H - 1
                                r = slice(quad * BANK, (quad + 1) * BANK)
                                dve.wait_ge(unit_high, at("unit_high", n, s["unit"] + 1))
                                dve.scalar_tensor_tensor(headT[1][:, h, r], unitP[s["unit"] % 2][:], bias_cols[:, 2, bass.ds(head, 1)],
                                                         headT[0][:, h, r].bitcast(F32), ALU.add,
                                                         ALU.subtract).then_inc(unit_low_done, 1)
                        invert()

                    dve.wait_ge(consts_in, 16)
                    with dve.Fori(0, B) as b:
                        for c in range(DC):
                            dve.wait_ge(xt_high, at("xt_high", b, c + 1))
                            dve.tensor_tensor(xT[1][:, c, :], slots[c][:], xT[0][:, c, :].bitcast(F32),
                                              ALU.subtract).then_inc(xt_low_done, 1)
                        dve.wait_ge(stream_in, b * 16 + 16)
                        run(b * PAIRS, STEPS, 0, b)
                        with dve.Fori(1, PAIRS) as g:
                            run(b * PAIRS + g, STEPS, g, b + 1)
                    run(B * PAIRS, TAIL, 0, B)

                @block.gpsimd
                def _(pool):
                    def split(n, nth, parts, raw, ready, arrived, count):
                        wait_alone(pool, passed, arrived, count)
                        pool.tensor_scalar(parts[0], raw, 1.0, 1.0, ALU.mult, ALU.mult).then_inc(w_high, 1)
                        pool.wait_ge(w_high, at("w_high", n, nth + 1))
                        pool.tensor_tensor(parts[1], raw, parts[0].bitcast(F32), ALU.subtract).then_inc(ready, 1)

                    def split_qk(n, nth, head, uses):
                        split(n, nth, [w[:].rearrange("p m c n -> p (m c n)") for w in wqk[head]],
                              raw_wqk[head][:].rearrange("p m c n -> p (m c n)"), wqk_ready[head], raw_qk[head], uses)

                    def divide(n, head, quad):
                        for i in range(4):
                            row = 8 * head + 4 * quad + i
                            keys = (4 * quad + i + 1) * P
                            r = probs[quad][:, i, 0:keys]
                            wait_alone(pool, passed, inverse_ready, at("inverse_ready", n, row + 1))
                            pool.tensor_scalar(r, r, inverse[:, row:row + 1], 1.0, ALU.mult, ALU.mult).then_inc(divided, 1)

                    k0 = next(s["slot"] for s in STEPS if s["kind"] == "k" and s["head"] == 0)
                    o1 = next(s["slot"] for s in STEPS if s["kind"] == "output" and s["j"] == 1)

                    def run(n):
                        split(n, 0, [w[:].rearrange("p c n -> p (c n)") for w in wv],
                              raw_wv[:].rearrange("p c n -> p (c n)"), wv_ready, raw_v, n * 16 + 16)
                        split_qk(n, 1, 1, n * 32 + 32)
                        divide(n, 0, 0)
                        pool.wait_ge(slot_full, at("slot_full", n, k0 + 1))
                        split_qk(n, 2, 0, n * 32 + 64)
                        pool.wait_ge(slot_full, at("slot_full", n, o1 + 1))
                        split(n, 3, [w[:].rearrange("p h n -> p (h n)") for w in wo],
                              raw_wo[:].rearrange("p h n -> p (h n)"), wo_ready, raw_o, n * 16 + 16)
                        divide(n, 0, 1)
                        divide(n, 1, 0)
                        divide(n, 1, 1)

                    pool.wait_ge(raw_qk[0], 32)
                    parts = [w[:].rearrange("p m c n -> p (m c n)") for w in wqk[0]]
                    raw = raw_wqk[0][:].rearrange("p m c n -> p (m c n)")
                    pool.tensor_scalar(parts[0], raw, 1.0, 1.0, ALU.mult, ALU.mult).then_inc(ident_ready, 1)
                    pool.wait_ge(ident_ready, 3)
                    pool.tensor_tensor(parts[1], raw, parts[0].bitcast(F32), ALU.subtract).then_inc(wqk_ready[0], 1)
                    with pool.Fori(0, B * PAIRS) as n:
                        run(n)

        feed_forward(nc, passed, stream, TB, ident, bo_rows, B, w_router, we_gate, we_up, we_down, ws_gate, ws_up, ws_down, out)


def feed_forward(nc, passed, stream, first, ident, bo_rows, B, w_router, we_gate, we_up, we_down, ws_gate, ws_up, ws_down, out):
    E, D, DE = we_gate.shape
    DS = ws_gate.shape[1]
    DC = D // P
    ROUTED = E * DE
    RC = ROUTED // P
    FT = ROUTED + DS
    CHUNKS = [(c * P, min(P, FT - c * P)) for c in range((FT + P - 1) // P)]
    NCH = len(CHUNKS)
    T = out.shape[1]
    NB = B * T // P
    TILE = 4 * P
    TILES = NB // 4
    EPS = 1e-5
    assert D == 2 * P and RC * P == ROUTED and NCH % 2 == 0 and E == 8

    with ExitStack() as st:
        def sb(name, shape, dt=F32):
            return st.enter_context(nc.sbuf_tensor(name, shape, dt))

        def sem(name):
            return st.enter_context(nc.semaphore(name))

        select = sb("select", [2 * E, ROUTED], F32R)
        sel_set, sel_low, sel_cut = sem("sel_set"), sem("sel_low"), sem("sel_cut")
        with nc.sbuf_tensor("band", [2 * E, 2, ROUTED], F32) as band, nc.Block() as block:
            @block.gpsimd
            def _(pool):
                flat = band[:].rearrange("p i f -> p (i f)")
                pool.memset(flat, 1.0).then_inc(sel_set, 1)
                pool.wait_ge(sel_set, 1)
                pool.affine_select(out=flat, in_=flat, compare_op=ALU.is_ge, fill=0.0, base=0,
                                   pattern=[[1, 2 * ROUTED]], channel_multiplier=-DE).then_inc(sel_low, 1)
                pool.wait_ge(sel_low, 1)
                pool.affine_select(out=flat, in_=flat, compare_op=ALU.is_ge, fill=0.0, base=DE - 1,
                                   pattern=[[-1, 2 * ROUTED]], channel_multiplier=DE).then_inc(sel_cut, 1)

            @block.vector
            def _(dve):
                dve.wait_ge(sel_cut, 1)
                dve.tensor_tensor(select[:], band[:, 0, :], band[:, 1, :], ALU.add)

        router = sb("router", [P, DC, E])
        raw = [sb(f"raw{i}", [P, FT if FT > 7 * D else 7 * D]) for i in range(2)]
        gate = [sb(f"gate_{p}", [P, DC, FT], F32R) for p in ("high", "low")]
        up = [sb(f"up_{p}", [P, DC, FT], F32R) for p in ("high", "low")]
        down = [sb(f"down_{p}", [P, NCH, D], F32R) for p in ("high", "low")]
        tokT = sb("tokT", [P, DC, TILE])
        tokT2 = [sb(f"tokT_{p}", [P, DC, TILE], F32R) for p in ("high", "low")]
        tok = sb("tok", [P, 4, D])
        stats = sb("stats", [P, 4, 6])
        moments = sb("moments", [P, 4, 2])
        spread = sb("spread", [P, 4])
        rstd = sb("rstd", [P, 4])
        neg_mean = sb("neg_mean", [P, 4])
        minus_half = sb("minus_half", [P, 4])
        logit = sb("logit", [P, NB, E])
        score = sb("score", [P, NB, E])
        pick = sb("pick", [P, NB, E])
        first_hot = sb("first_hot", [P, NB, E])
        rest = sb("rest", [P, NB, E])
        order = sb("order", [P, E])
        best = sb("best", [P, NB])
        total = sb("total", [P, NB])
        mix = sb("mix", [P, NB, 2 * E])
        mix_high = sb("mix_high", [P, NB, E], F32R)
        tok_mix = sb("tok_mix", [P, 4, 2 * E])
        mixT = sb("mixT", [2 * E, TILE], F32R)
        silu = [sb(f"silu{i}", [P, TILE]) for i in range(2)]
        both = [sb(f"both{i}", [P, TILE]) for i in range(2)]
        hid = [sb(f"hid{i}", [P, TILE]) for i in range(2)]
        hid2 = [[sb(f"hid{i}_{p}", [P, TILE], F32R) for p in ("high", "low")] for i in range(2)]
        summed = sb("summed", [P, 4, D])
        result = sb("result", [P, 4, D])

        guP = st.enter_context(nc.psum_tensor("guP", [P, 2, BANK], F32))
        mixP = st.enter_context(nc.psum_tensor("mixP", [P, BANK], F32))
        logitP = st.enter_context(nc.psum_tensor("logitP", [P, 4, E], F32))
        yP = st.enter_context(nc.psum_tensor("yP", [P, 4, BANK], F32))

        consts, w_in = sem("ffn_consts"), [sem(f"w_in{i}") for i in range(2)]
        w_high, w_low = sem("ffn_w_high"), sem("ffn_w_low")
        ready, chain = sem("half_ready"), sem("dve_chain")
        res_sum, stat_done, mom_done, normed = (sem(n) for n in ("res_sum", "stat_done", "mom_done", "normed"))
        spread_done, rstd_done = sem("spread_done"), sem("rstd_done")
        turned1, tokT_done, logits_full, logits_kept = (sem(n) for n in ("turned1", "tokT_done", "logits_full", "logits_kept"))
        exp_in, exp_out, mixed = sem("exp_in"), sem("exp_out"), sem("mixed")

        def pieces():
            for w, c in ((gate, 0), (gate, 1), (up, 0), (up, 1)):
                yield [(w, slice(0, P), (slice(None), c), 0, FT)]
            yield [(down, slice(0, P), (slice(None), slice(0, 7)), 0, 7 * D)]
            full = NCH - 8
            yield [(down, slice(0, P), (slice(None), slice(7, NCH - 1)), 0, full * D),
                   (down, slice(0, CHUNKS[-1][1]), (slice(None), NCH - 1), full * D, (full + 1) * D)]

        PIECES = list(pieces())
        LOADS = [2, 2, 2, 2, 1, 3]

        def piece_view(parts, part, rows, where):
            v = parts[part][(rows,) + tuple(where[1:])]
            return v

        def raw_view(i, rows, where, lo, hi):
            v = raw[i % 2][rows, lo:hi]
            if isinstance(where[1], slice):
                v = v.rearrange("p (c d) -> p c d", d=D)
            return v

        with nc.Block() as block:
            @block.sync
            def _(sp):
                sp.dma_start(router[:], w_router.rearrange("(c p) e -> p c e", p=P)).then_inc(consts, 16)
                for i in range(len(PIECES)):
                    if i >= 2:
                        sp.wait_ge(w_low, sum(len(x) for x in PIECES[:i - 1]))
                    s, buf = w_in[i % 2], raw[i % 2]
                    if i < 4:
                        routed, shared = ((we_gate, ws_gate), (we_up, ws_up))[i // 2]
                        r = slice((i % 2) * P, (i % 2 + 1) * P)
                        sp.dma_start(buf[:, 0:ROUTED].rearrange("p (e f) -> p e f", e=E),
                                     routed[:, r, :].rearrange("e p f -> p e f")).then_inc(s, 16)
                        sp.dma_start(buf[:, ROUTED:FT], shared[r, :]).then_inc(s, 16)
                    else:
                        flat = we_down.rearrange("e f d -> (e f) d")
                        if i == 4:
                            sp.dma_start(buf[:, 0:7 * D].rearrange("p (c d) -> p c d", d=D),
                                         flat[0:7 * P].rearrange("(c p) d -> p c d", p=P)).then_inc(s, 16)
                        else:
                            nr, ns = RC - 7, DS // P
                            sp.dma_start(buf[:, 0:nr * D].rearrange("p (c d) -> p c d", d=D),
                                         flat[7 * P:ROUTED].rearrange("(c p) d -> p c d", p=P)).then_inc(s, 16)
                            sp.dma_start(buf[:, nr * D:(nr + ns) * D].rearrange("p (c d) -> p c d", d=D),
                                         ws_down[0:ns * P].rearrange("(c p) d -> p c d", p=P)).then_inc(s, 16)
                            sp.dma_start(buf[0:DS - ns * P, (nr + ns) * D:(nr + ns + 1) * D],
                                         ws_down[ns * P:DS]).then_inc(s, 16)

            @block.gpsimd
            def _(pool):
                pool.memset(minus_half[:], -0.5).then_inc(ready, 1)
                for e in range(E):
                    made = pool.memset(order[:, e:e + 1], float(E - e))
                made.then_inc(ready, 1)
                pool.wait_ge(ready, 1)
                for j in range(TILES):
                    pool.wait_ge(mom_done, j + 1)
                    pool.tensor_scalar(spread[:], moments[:, :, 1], EPS, 1.0, ALU.add, ALU.mult).then_inc(spread_done, 1)
                    pool.wait_ge(spread_done, j + 1)
                    pool.tensor_tensor(rstd[:], spread[:], minus_half[:], ALU.pow).then_inc(rstd_done, 1)

            @block.vector
            def _(dve):
                made_low = 0
                for j in range(TILES + 1):
                    if j < TILES:
                        x = stream[:, first + 4 * j:first + 4 * j + 4, :]
                        dve.tensor_tensor(x, x, bo_rows[:].unsqueeze(1).to_broadcast([P, 4, D]), ALU.add).then_inc(res_sum, 1)
                        dve.wait_ge(res_sum, j + 1)
                        for t in range(4):
                            made = dve.bn_stats(stats[:, t, :], x[:, t, :])
                        made.then_inc(stat_done, 1)
                        dve.wait_ge(stat_done, j + 1)
                        for t in range(4):
                            made = dve.bn_aggr(moments[:, t, :], stats[:, t, :])
                        made.then_inc(mom_done, 1)
                    if 1 <= j <= len(PIECES):
                        for parts, rows, where, lo, hi in PIECES[j - 1]:
                            made_low += 1
                            dve.wait_ge(w_high, made_low)
                            dve.tensor_tensor(piece_view(parts, 1, rows, where), raw_view(j - 1, rows, where, lo, hi),
                                              piece_view(parts, 0, rows, where).bitcast(F32), ALU.subtract).then_inc(w_low, 1)
                    if j < TILES:
                        dve.wait_ge(rstd_done, j + 1)
                        for t in range(4):
                            made = dve.tensor_scalar(x[:, t, :], x[:, t, :], moments[:, t, 0:1], rstd[:, t:t + 1],
                                                     ALU.subtract, ALU.mult)
                        made.then_inc(normed, 1)

                n = [0]

                def link(made):
                    n[0] += 1
                    made.then_inc(chain, 1)
                    dve.wait_ge(chain, n[0])

                def over_experts(a):
                    return a[:].unsqueeze(2).to_broadcast([P, NB, E])

                def first_of_equal(dst, values, largest):
                    link(dve.tensor_tensor(dst[:], values[:], over_experts(largest), ALU.is_equal))
                    link(dve.tensor_tensor(dst[:], dst[:], order[:].unsqueeze(1).to_broadcast([P, NB, E]), ALU.mult))
                    link(dve.reduce_max(largest[:], dst[:], AX.X))
                    link(dve.tensor_tensor(dst[:], dst[:], over_experts(largest), ALU.is_equal))

                dve.wait_ge(logits_kept, TILES)
                dve.wait_ge(ready, 2)
                link(dve.reduce_max(best[:], logit[:], AX.X))
                dve.tensor_tensor(score[:], logit[:], over_experts(best), ALU.subtract).then_inc(exp_in, 1)
                dve.wait_ge(exp_out, 1)
                link(dve.reduce_sum(total[:], score[:], AX.X))
                link(dve.reciprocal(total[:], total[:]))
                link(dve.tensor_tensor(score[:], score[:], over_experts(total), ALU.mult))
                link(dve.reduce_max(best[:], score[:], AX.X))
                first_of_equal(first_hot, score, best)
                link(dve.scalar_tensor_tensor(rest[:], first_hot[:], -4.0, score[:], ALU.mult, ALU.add))
                link(dve.reduce_max(best[:], rest[:], AX.X))
                first_of_equal(pick, rest, best)
                link(dve.tensor_tensor(pick[:], pick[:], first_hot[:], ALU.add))
                link(dve.tensor_tensor(score[:], score[:], pick[:], ALU.mult))
                link(dve.tensor_copy(mix_high[:], score[:]))
                link(dve.tensor_copy(mix[:, :, 0:E], mix_high[:].bitcast(F32)))
                link(dve.tensor_tensor(mix[:, :, E:2 * E], score[:], mix_high[:].bitcast(F32), ALU.subtract))

            @block.tensor
            def _(pe):
                pe.wait_ge(consts, 16)
                for j in range(TILES):
                    pe.wait_ge(normed, j + 1)
                    if j:
                        pe.wait_ge(tokT_done, j)
                    for c in range(DC):
                        for t in range(4):
                            made = pe.transpose(guP[:, c, t * P:(t + 1) * P],
                                                stream[:, first + 4 * j + t, c * P:(c + 1) * P], ident[:])
                    made.then_inc(turned1, 1)
                    pe.wait_ge(tokT_done, j + 1)
                    if j:
                        pe.wait_ge(logits_kept, j)
                    for t in range(4):
                        for c in range(DC):
                            made = pe.matmul(logitP[:, t, :], tokT[:, c, t * P:(t + 1) * P], router[:, c, :],
                                             start=c == 0, stop=c == DC - 1)
                    made.then_inc(logits_full, 1)

            @block.scalar
            def _(act):
                def high(i):
                    act.wait_ge(w_in[i % 2], 16 * sum(LOADS[k] for k in range(i % 2, i + 1, 2)))
                    for parts, rows, where, lo, hi in PIECES[i]:
                        act.activation(piece_view(parts, 0, rows, where), raw_view(i, rows, where, lo, hi),
                                       ACT.Copy).then_inc(w_high, 1)

                for j in range(TILES):
                    if j < len(PIECES):
                        high(j)
                    act.wait_ge(turned1, j + 1)
                    act.activation(tokT[:], guP[:], ACT.Copy).then_inc(tokT_done, 1)
                    act.wait_ge(logits_full, j + 1)
                    act.activation(logit[:, 4 * j:4 * j + 4, :], logitP[:], ACT.Copy).then_inc(logits_kept, 1)
                act.wait_ge(exp_in, 1)
                act.activation(score[:], score[:], ACT.Exp).then_inc(exp_out, 1)

        counts = {}

        def counted(name, n):
            counts[name] = (sem(name), n)
            return counts[name][0]

        def at(name, j, i):
            return j * counts[name][1] + counts[name][1] + i

        tok_staged = counted("tok_staged", 1)
        tok_turned = counted("tok_turned", 1)
        tok_high = counted("tok_high", 1)
        tok_low = counted("tok_low", 1)
        gate_full = counted("gate_full", NCH)
        up_full = counted("up_full", NCH)
        silu_done = counted("silu_done", NCH)
        both_done = counted("both_done", RC)
        hid_done = counted("hid_done", NCH)
        hid_high = counted("hid_high", NCH)
        hid_low = counted("hid_low", NCH)
        down_full = counted("down_full", 1)
        y_added = counted("y_added", 1)
        stats2 = counted("stats2", 1)
        moments2 = counted("moments2", 1)
        spread2 = counted("spread2", 2)
        rstd2 = counted("rstd2", 1)
        result_done = counted("result_done", 1)
        stored = counted("stored", 16)

        with nc.Block() as block:
            @block.gpsimd
            def _(pool):
                for s, n in counts.values():
                    pool.sem_inc(s, n)

        with nc.Block() as block:
            @block.sync
            def _(sp):
                flat = out.rearrange("b (t p) d -> p (b t) d", p=P)
                with sp.Fori(0, TILES) as j:
                    sp.wait_ge(result_done, at("result_done", j, 1))
                    sp.dma_start(flat[:, bass.ds(j * 4, 4), :], result[:]).then_inc(stored, 16)
                sp.wait_ge(stored, 16 * (TILES + 1))

            @block.tensor
            def _(pe):
                def hidden(dst, w, c):
                    lo, m = CHUNKS[c]
                    for k in range(DC):
                        for i, (x, y) in enumerate(((1, 0), (0, 0), (0, 1))):
                            made = pe.matmul(dst[0:m], w[x][:, k, lo:lo + m], tokT2[y][:, k, :],
                                             start=k == 0 and i == 0, stop=k == DC - 1 and i == 2)
                    return made

                def project_down(j, c):
                    m = CHUNKS[c][1]
                    pe.wait_ge(hid_low, at("hid_low", j, c + 1))
                    for t in range(4):
                        for i, (x, y) in enumerate(((1, 0), (0, 0), (0, 1))):
                            made = pe.matmul(yP[:, t, 0:D], hid2[c % 2][x][0:m, t * P:(t + 1) * P], down[y][0:m, c, :],
                                             start=c == 0 and i == 0, stop=c == NCH - 1 and i == 2)
                    return made

                with pe.Fori(0, TILES) as j:
                    pe.wait_ge(tok_staged, at("tok_staged", j, 1))
                    pe.wait_ge(hid_done, at("hid_done", j, 0))
                    for c in range(DC):
                        for t in range(4):
                            pe.transpose(guP[:, c, t * P:(t + 1) * P], tok[:, t, c * P:(c + 1) * P], ident[:])
                    for t in range(4):
                        made = pe.transpose(mixP[0:2 * E, t * P:(t + 1) * P], tok_mix[:, t, :], ident[:])
                    made.then_inc(tok_turned, 1)
                    pe.wait_ge(tok_low, at("tok_low", j, 1))
                    for c in range(NCH):
                        if c:
                            pe.wait_ge(silu_done, at("silu_done", j, c))
                        hidden(guP[:, 0, :], gate, c).then_inc(gate_full, 1)
                        if c:
                            pe.wait_ge(hid_done, at("hid_done", j, c))
                        made = hidden(guP[:, 1, :], up, c)
                        if c < RC:
                            made = pe.matmul(mixP[:], select[:, c * P:(c + 1) * P], mixT[:], start=True, stop=True)
                        made.then_inc(up_full, 1)
                        if c == 1:
                            pe.wait_ge(y_added, at("y_added", j, 0))
                        if c:
                            project_down(j, c - 1)
                    project_down(j, NCH - 1).then_inc(down_full, 1)

            @block.scalar
            def _(act):
                with act.Fori(0, TILES) as j:
                    wait_alone(act, passed, tok_turned, at("tok_turned", j, 0))
                    act.activation(tok[:], stream[:, bass.ds(j * 4 + first, 4), :], ACT.Copy)
                    act.activation(tok_mix[:], mix[:, bass.ds(j * 4, 4), :], ACT.Copy).then_inc(tok_staged, 1)
                    act.wait_ge(tok_turned, at("tok_turned", j, 1))
                    act.activation(tokT2[0][:], guP[:], ACT.Copy).then_inc(tok_high, 1)
                    for c in range(NCH):
                        m = CHUNKS[c][1]
                        act.wait_ge(gate_full, at("gate_full", j, c + 1))
                        act.activation(silu[c % 2][0:m], guP[0:m, 0, :], ACT.Silu).then_inc(silu_done, 1)
                        act.wait_ge(hid_done, at("hid_done", j, c + 1))
                        act.activation(hid2[c % 2][0][0:m], hid[c % 2][0:m], ACT.Copy).then_inc(hid_high, 1)

            @block.vector
            def _(dve):
                with dve.Fori(0, TILES) as j:
                    dve.wait_ge(tok_high, at("tok_high", j, 1))
                    dve.tensor_tensor(tokT2[1][:], guP[:], tokT2[0][:].bitcast(F32), ALU.subtract)
                    dve.tensor_copy(mixT[:], mixP[0:2 * E, :]).then_inc(tok_low, 1)
                    for c in range(NCH):
                        m = CHUNKS[c][1]
                        dve.wait_ge(silu_done, at("silu_done", j, c + 1))
                        dve.wait_ge(up_full, at("up_full", j, c + 1))
                        if c < RC:
                            dve.tensor_tensor(both[c % 2][:], guP[:, 1, :], silu[c % 2][:], ALU.mult).then_inc(both_done, 1)
                            dve.wait_ge(both_done, at("both_done", j, c + 1))
                            dve.tensor_tensor(hid[c % 2][:], mixP[:], both[c % 2][:], ALU.mult).then_inc(hid_done, 1)
                        else:
                            dve.tensor_tensor(hid[c % 2][0:m], guP[0:m, 1, :], silu[c % 2][0:m], ALU.mult).then_inc(hid_done, 1)
                        dve.wait_ge(hid_high, at("hid_high", j, c + 1))
                        dve.tensor_tensor(hid2[c % 2][1][0:m], hid[c % 2][0:m], hid2[c % 2][0][0:m].bitcast(F32),
                                          ALU.subtract).then_inc(hid_low, 1)
                    dve.wait_ge(down_full, at("down_full", j, 1))
                    dve.wait_ge(result_done, at("result_done", j, 0))
                    dve.tensor_tensor(summed[:], yP[:, :, 0:D], stream[:, bass.ds(j * 4 + first, 4), :], ALU.add).then_inc(y_added, 1)
                    dve.wait_ge(y_added, at("y_added", j, 1))
                    for t in range(4):
                        made = dve.bn_stats(stats[:, t, :], summed[:, t, :])
                    made.then_inc(stats2, 1)
                    wait_alone(dve, passed, stats2, at("stats2", j, 1))
                    for t in range(4):
                        made = dve.bn_aggr(moments[:, t, :], stats[:, t, :])
                    made.then_inc(moments2, 1)

            @block.gpsimd
            def _(pool):
                with pool.Fori(0, TILES) as j:
                    wait_alone(pool, passed, moments2, at("moments2", j, 1))
                    pool.tensor_scalar(neg_mean[:], moments[:, :, 0], -1.0, 1.0, ALU.mult, ALU.mult).then_inc(spread2, 1)
                    pool.tensor_scalar(spread[:], moments[:, :, 1], EPS, 1.0, ALU.add, ALU.mult).then_inc(spread2, 1)
                    pool.wait_ge(spread2, at("spread2", j, 2))
                    pool.tensor_tensor(rstd[:], spread[:], minus_half[:], ALU.pow).then_inc(rstd2, 1)
                    pool.wait_ge(rstd2, at("rstd2", j, 1))
                    wait_alone(pool, passed, stored, at("stored", j, 0))
                    for t in range(4):
                        made = pool.tensor_scalar(result[:, t, :], summed[:, t, :], neg_mean[:, t:t + 1], rstd[:, t:t + 1],
                                                  ALU.add, ALU.mult)
                    made.then_inc(result_done, 1)


_INS = ["L0_attn_query", "L0_attn_w_q", "L0_attn_b_q", "L0_attn_w_k", "L0_attn_b_k", "L0_attn_w_v", "L0_attn_b_v",
        "L0_attn_w_o", "L0_attn_b_o", "L0_ffn_W_router", "L0_ffn_We_gate", "L0_ffn_We_up", "L0_ffn_We_down",
        "L0_ffn_Ws_gate", "L0_ffn_Ws_up", "L0_ffn_Ws_down"]


def kernel(**inputs):
    import numpy as _np
    import concourse.bacc as _bacc
    from concourse import mybir as _mybir
    from concourse.bass_utils import run_bass_kernel_spmd as _run

    nc = _bacc.Bacc("TRN2", target_bir_lowering=False, num_devices=1)
    arrays, args = {}, []
    for name in _INS:
        a = _np.ascontiguousarray(inputs[name])
        arrays[f"in_{name}"] = a
        args.append(nc.dram_tensor(f"in_{name}", a.shape, _mybir.dt.from_np(a.dtype), kind="ExternalInput").ap())
    shape = inputs["L0_attn_query"].shape
    res = nc.dram_tensor("out", shape, _mybir.dt.float32, kind="ExternalOutput")
    layer(nc, *args, res.ap())
    r = _run(nc, [arrays], core_ids=[0])
    return r.results[0]["out"]
```

```python
from contextlib import ExitStack

import concourse.bass as bass
from concourse import mybir

F32 = mybir.dt.float32
F32R = mybir.dt.float32r
ALU = mybir.AluOpType
ACT = mybir.ActivationFunctionType
AX = mybir.AxisListType

P = 128
BANK = 512


def wait_alone(engine, passed, signal, count):
    engine.wait_ge(signal, count)
    engine.sem_inc(passed, 1)


TENSOR_ORDER = (
    "t t t s s q1a p p t p q1b t s s p t k1a p t t v0 s v1 p p t p k1b v2 t o0a s s p t p",
    "s p t o0b v3 p o1a s t t t q2a p t p s s t p o1b s p t t p t s p s p t p s t s t p",
    "q2b k2a t k2b p p p",
)
BANKS = 4
TURN_BUFFERS = 3
SCALAR_LAG = {"x": 0, "q": 1.5, "k": 1.5, "v": 1.5, "score": 4.0, "turn": 1.5, "unit_end": 1.0}
VECTOR_LAG = {"x": 0.5, "q": 3.5, "k": 3.5, "v": 3.5, "o": 2.0, "score": 1.0, "inverse": 6.0, "turn": 3.0, "unit_end": 3.0}


def first_column(s):
    return min(max(s["kb"] - 4 * s["quad"], 0), 2) * P


def attention_schedule(refresh=False):
    count = {"slot_full": 0, "proj_low_done": 0, "exp_done": 0, "turn": 0, "unit": 0, "output_added": 0}

    def take(kind):
        count[kind] += 1
        return count[kind] - 1

    scored = [(h, g, i) for h in range(2) for g in range(2) for i in range(4)]
    units = [(1, 1), (0, 0), (0, 1), (1, 0)]
    blocks = [(u, kb) for u, (_, g) in enumerate(units) for kb in range(4 * g + 4)]
    first_turn = [blocks.index((u, 0)) for u in range(4)]
    steps, products = [], 0
    for word in " ".join(TENSOR_ORDER).split():
        if word == "s":
            row = take("exp_done")
            h, g, i = scored[row]
            s = dict(kind="score", head=h, quad=g, i=i, row=row, frees=("exp_done", row + 1))
        elif word in "tp":
            nth = take("turn") if word == "t" else products
            products += word == "p"
            u, kb = blocks[nth]
            h, g = units[u]
            s = dict(kind="turn" if word == "t" else "pv", head=h, quad=g, kb=kb, turn=nth, unit=u,
                     row=4 * u, last=kb == 4 * g + 3)
        else:
            s = dict(kind=word[0], head=int(word[1]) if word[0] in "qk" else 0, part="ab".find(word[2:]) if word[0] != "v" else int(word[1]))
            if word[0] == "o":
                nth = take("output_added")
                s.update(j=nth, frees=("output_added", nth + 1))
            else:
                nth = take("proj_low_done")
                s.update(proj=nth, frees=("proj_low_done", nth + 1))
        if "frees" in s:
            s["full"] = take("slot_full")
        steps.append(s)
    count["unit"] = len(units)

    used = [-BANKS + i for i in range(BANKS)]
    for s in steps:
        if "frees" in s:
            size = 2 if s["kind"] == "score" and s["quad"] == 1 else 1
            s["bank"] = min(range(0, BANKS, size), key=lambda k: max(used[k:k + size]))
            s["banks"] = size
            used[s["bank"]:s["bank"] + size] = [s["full"]] * size
    if refresh:
        at = next(k for k, s in enumerate(steps) if s["kind"] == "q" and s["head"] == 2)
        steps[at:at] = [dict(kind="x", c=c, bank=2 * c, banks=2, frees=("xt_low_done", c + 1)) for c in range(2)]

    last = {}
    for lap in range(2):
        for s in steps:
            if "frees" in s:
                mine = range(s["bank"], s["bank"] + s["banks"])
                s["free"] = {}
                for k in mine:
                    if k in last:
                        (name, nth), of_lap = last[k]
                        nth -= count.get(name, 0) * (lap - of_lap)
                        s["free"][name] = max(s["free"].get(name, nth), nth)
                    last[k] = (s["frees"], lap)
    return steps, count


def scalar_order(steps):
    items = [(k + SCALAR_LAG[s["kind"]], s["kind"], s) for k, s in enumerate(steps) if s["kind"] in SCALAR_LAG]
    items += [(k + SCALAR_LAG["unit_end"], "unit_end", s) for k, s in enumerate(steps) if s["kind"] == "pv" and s["last"]]
    return [item[1:] for item in sorted(items, key=lambda item: item[0])]


def vector_order(steps):
    items = [(k + VECTOR_LAG[s["kind"]], s["kind"], s) for k, s in enumerate(steps) if s["kind"] in VECTOR_LAG]
    items += [(k + VECTOR_LAG["inverse"], "inverse", s) for k, s in enumerate(steps) if s["kind"] == "score"]
    items += [(k + VECTOR_LAG["unit_end"], "unit_end", s) for k, s in enumerate(steps) if s["kind"] == "pv" and s["last"]]
    return [item[1:] for item in sorted(items, key=lambda item: item[0])]


def layer(nc, query, w_q, b_q, w_k, b_k, w_v, b_v, w_o, b_o, w_router, we_gate, we_up, we_down,
          ws_gate, ws_up, ws_down, out):
    B, T, D = query.shape
    HD = P
    H = w_q.shape[1] // HD
    PAIRS = H // 2
    DC = D // P
    TB = T // P
    NB = B * TB
    E, _, DE = we_gate.shape
    DS = ws_gate.shape[1]
    ROUTED = E * DE
    RC = ROUTED // P
    FT = ROUTED + DS
    CHUNKS = [(c * P, min(P, FT - c * P)) for c in range((FT + P - 1) // P)]
    NCH = len(CHUNKS)
    TILE = 4 * P
    TILES = B * T // TILE
    assert (D, TB, HD) == (2 * P, 8, P) and ROUTED == RC * P and H % 2 == 0
    SCALE = float(HD) ** -0.5
    MASKED = -1e10 / SCALE
    EPS = 1e-5

    STEPS, COUNT = attention_schedule()
    LAST_STEPS, _ = attention_schedule(refresh=True)
    SLOTS, ROWS, TURNS, UNITS, PROJ, OUTS = (
        COUNT[k] for k in ("slot_full", "exp_done", "turn", "unit", "proj_low_done", "output_added"))
    TAIL = [s for s in STEPS if s["kind"] in ("turn", "pv") and s["unit"] == 0]
    TAIL += [dict(s, full=k, bank=k, banks=1, free={"exp_done": 0, "proj_low_done": 0, "output_added": 0})
             for k, s in enumerate(s for s in STEPS if s["kind"] == "o")]
    X_STEPS = [s for s in LAST_STEPS if s["kind"] == "x"]
    HEAD = [dict(s, head=0, full=k - 4, proj=k - 4, bank=k, banks=1, free={})
            for k, s in enumerate(s for s in STEPS if s["head"] == 2 and s["kind"] in "qk")]
    BEFORE = [dict(s, free={}) for s in X_STEPS] + HEAD

    def nth_full(kinds, head=None):
        return 1 + max(s["full"] for s in STEPS if s["kind"] in kinds and head in (None, s["head"]))

    def nth_proj(kind, head, part):
        return 1 + next(s["proj"] for s in STEPS if (s["kind"], s["head"], s["part"] if "part" in s else None) == (kind, head, part))

    ctx = ExitStack()
    with ctx:
        def sem(name):
            return ctx.enter_context(nc.semaphore(name))

        totals = {}

        def counted(name, total):
            s = sem(name)
            totals[name] = (s, total)
            return s

        slot_full = counted("slot_full", SLOTS)
        turned = counted("turned", TURNS)
        pv_done = counted("pv_done", TURNS)
        exp_done = counted("exp_done", ROWS)
        turn_high = counted("turn_high", TURNS)
        unit_high = counted("unit_high", UNITS)
        proj_high = counted("proj_high", PROJ)
        part_max = counted("part_max", ROWS)
        shift_ready = counted("shift_ready", ROWS)
        inverse_ready = counted("inverse_ready", ROWS)
        turn_low_done = counted("turn_low_done", TURNS)
        unit_low_done = counted("unit_low_done", UNITS)
        proj_low_done = counted("proj_low_done", PROJ)
        output_added = counted("output_added", OUTS)
        divided = counted("divided", ROWS)
        w_high = counted("w_high", 4)
        wv_ready = counted("wv_ready", 1)
        wqk_ready = [counted(f"wqk{h}_ready", 1) for h in range(2)]
        wo_ready = counted("wo_ready", 1)
        raw_qk = [sem(f"raw_qk{h}") for h in range(2)]
        raw_v = sem("raw_v")
        raw_o = sem("raw_o")
        xt_full = counted("xt_full", DC)
        xt_high = counted("xt_high", DC)
        xt_low_done = counted("xt_low_done", DC)
        x_staged = sem("x_staged")
        consts_in = sem("consts_in")
        bias_in = sem("bias_in")
        bias_turned = sem("bias_turned")
        stream_in = sem("stream_in")
        passed = sem("passed")
        ident_zero = sem("ident_zero")
        ident_ready = sem("ident_ready")
        free_event = {"proj_low_done": proj_low_done, "exp_done": exp_done, "output_added": output_added,
                      "xt_low_done": xt_low_done}

        def at(name, n, i):
            return n * totals[name][1] + totals[name][1] + i

        def head_at(n, i):
            if isinstance(n, int):
                return slice((2 * n + i + H) % H, (2 * n + i + H) % H + 1)
            return bass.ds((n * 2 + (i + H)) % H, 1)

        def stream_block(n):
            return (n + PAIRS - 1) // PAIRS * TB

        def sb(stack, name, shape, dt=F32):
            return stack.enter_context(nc.sbuf_tensor(name, shape, dt))

        stream = sb(ctx, "stream", [P, (B + 1) * TB, D])
        ident = sb(ctx, "ident", [P, P])
        bo_rows = sb(ctx, "bo_rows", [P, D])

        with ExitStack() as st:
            maskneg = sb(st, "maskneg", [P, P])
            bias_cols = sb(st, "bias_cols", [P, 3, H])
            bias_rows = sb(st, "bias_rows", [3 * H, HD])
            x_stage = sb(st, "x_stage", [P, TB, D])
            xT = [sb(st, f"xT_{p}", [P, DC, T], F32R) for p in ("high", "low")]
            raw_wqk = [sb(st, f"raw_wqk{h}", [P, 2, DC, HD]) for h in range(2)]
            raw_wv = sb(st, "raw_wv", [P, DC, 2 * HD])
            raw_wo = sb(st, "raw_wo", [P, 2, D])
            wqk = [[sb(st, f"wqk{h}_{p}", [P, 2, DC, HD], F32R) for p in ("high", "low")] for h in range(2)]
            wv = [sb(st, f"wv_{p}", [P, DC, 2 * HD], F32R) for p in ("high", "low")]
            wo = [sb(st, f"wo_{p}", [P, 2, D], F32R) for p in ("high", "low")]
            qT = [[sb(st, f"qT{h}_{p}", [P, T], F32R) for p in ("high", "low")] for h in range(2)]
            kT = [[sb(st, f"kT{h}_{p}", [P, T], F32R) for p in ("high", "low")] for h in range(2)]
            v = [sb(st, f"v_{p}", [P, TB, 2 * HD], F32R) for p in ("high", "low")]
            probs = [sb(st, f"probs{g}", [P, 4, 4 * (g + 1) * P]) for g in range(2)]
            probsT = [[sb(st, f"probsT{i}_{p}", [P, 4 * P], F32R) for p in ("high", "low")] for i in range(TURN_BUFFERS)]
            headT = [sb(st, f"headT_{p}", [P, 2, T], F32R) for p in ("high", "low")]
            row_max = sb(st, "row_max", [P, 2, ROWS])
            shift = sb(st, "shift", [P, ROWS])
            row_sum = sb(st, "row_sum", [P, ROWS])
            inverse = sb(st, "inverse", [P, ROWS])

            banks = st.enter_context(nc.psum_tensor("banks", [P, BANKS * BANK], F32))
            turnP = [st.enter_context(nc.psum_tensor(f"turnP{i}", [P, BANK], F32)) for i in range(TURN_BUFFERS)]
            unitP = st.enter_context(nc.psum_tensor("unitP", [P, BANK], F32))

            def slot_of(s):
                return banks[:, s["bank"] * BANK:(s["bank"] + s["banks"]) * BANK]

            def buffer_of(s):
                return s["turn"] % TURN_BUFFERS

            with nc.Block() as block:
                @block.sync
                def _(sp):
                    for m, bias in enumerate((b_q, b_k, b_v)):
                        sp.dma_start(bias_rows[m * H:(m + 1) * H, :], bias.rearrange("(h d) -> h d", d=HD)).then_inc(bias_in, 16)

                @block.tensor
                def _(pe):
                    pe.wait_ge(bias_in, 3 * 16)
                    pe.wait_ge(ident_ready, 1)
                    pe.transpose(turnP[0][:, 0:3 * H], bias_rows[:], ident[0:3 * H, 0:3 * H]).then_inc(bias_turned, 1)

                @block.scalar
                def _(act):
                    act.wait_ge(bias_turned, 1)
                    act.activation(bias_cols[:].rearrange("p m h -> p (m h)"), turnP[0][:, 0:3 * H], ACT.Copy)

                @block.gpsimd
                def _(pool):
                    pool.memset(ident[:], 0.0).then_inc(ident_zero, 1)
                    pool.memset(maskneg[:], 0.0).then_inc(ident_zero, 1)
                    pool.wait_ge(ident_zero, 2)
                    pool.affine_select(out=ident[:], in_=ident[:], compare_op=ALU.not_equal, fill=1.0, base=0,
                                       pattern=[[-1, P]], channel_multiplier=1).then_inc(ident_ready, 1)
                    pool.affine_select(out=maskneg[:], in_=maskneg[:], compare_op=ALU.is_ge, fill=MASKED, base=0,
                                       pattern=[[-1, P]], channel_multiplier=1).then_inc(ident_ready, 1)
                    for part in range(2):
                        pool.memset(wo[part][:].bitcast(F32), 0.0)
                        pool.memset(v[part][:].bitcast(F32), 0.0)
                    pool.wait_ge(ident_ready, 2)
                    done = dict(slot_full=len(HEAD), proj_high=len(HEAD), proj_low_done=len(HEAD),
                                w_high=3, wv_ready=1, wqk0_ready=1, wqk1_ready=1)
                    for name, (s, total) in totals.items():
                        if total > done.get(name, 0):
                            pool.sem_inc(s, total - done.get(name, 0))

                @block.vector
                def _(dve):
                    for g in range(2):
                        dve.memset(probs[g][:], 0.0)
                    for part in range(2):
                        dve.memset(headT[part][:].bitcast(F32), 0.0)
                    dve.memset(stream[:, 0:TB, :], 0.0)

            with nc.Block() as block:
                @block.sync
                def _(sp):
                    w_of = {"q": w_q, "k": w_k}

                    def load_qk(head, pair):
                        for m, w in enumerate((w_q, w_k)):
                            sp.dma_start(raw_wqk[head][:, m],
                                         w.rearrange("(c p) n -> p c n", p=P)[:, :, bass.ds(pair * 2 * HD + head * HD, HD)]
                                         ).then_inc(raw_qk[head], 16)

                    def load_v(pair):
                        sp.dma_start(raw_wv[:], w_v.rearrange("(c p) n -> p c n", p=P)[:, :, bass.ds(pair * 2 * HD, 2 * HD)]
                                     ).then_inc(raw_v, 16)

                    def load_x(b):
                        sp.dma_start(x_stage[:], query[bass.ds(b, 1)].rearrange("o (t p) d -> p (o t) d", p=P)
                                     ).then_inc(x_staged, 16)

                    load_qk(0, 0)
                    load_x(0)
                    load_v(0)
                    load_qk(1, 0)
                    sp.dma_start(bo_rows[:], b_o.rearrange("(o d) -> o d", o=1).to_broadcast([P, D])).then_inc(consts_in, 16)

                    def loads(n, pair, after):
                        sp.wait_ge(wqk_ready[0], at("wqk0_ready", n, 0))
                        load_qk(0, after)
                        sp.wait_ge(wv_ready, at("wv_ready", n, 0))
                        load_v(after)
                        sp.wait_ge(wo_ready, at("wo_ready", n, 0))
                        sp.dma_start(raw_wo[:], w_o.rearrange("(g h d) n -> d (g h) n", h=2, d=HD)[:, bass.ds(pair * 2, 2), :]
                                     ).then_inc(raw_o, 16)
                        sp.wait_ge(wqk_ready[1], at("wqk1_ready", n, 0))
                        load_qk(1, after)

                    with sp.Fori(0, B) as b:
                        loads(b * PAIRS, 0, 1)
                        sp.dma_start(stream[:, bass.ds((b + 1) * TB, TB), :],
                                     query[bass.ds(b, 1)].rearrange("o (t p) d -> p (o t) d", p=P)).then_inc(stream_in, 16)
                        sp.wait_ge(xt_full, at("xt_full", b, DC))
                        load_x((b + 1) % B)
                        with sp.Fori(1, PAIRS) as g:
                            loads(b * PAIRS + g, g, (g + 1) % PAIRS)
                    sp.wait_ge(x_staged, 16 * (B + 1))

                @block.tensor
                def _(pe):
                    def three(dst, a, b, ra, rb, first, last):
                        for j, (x, y) in enumerate(((1, 0), (0, 0), (0, 1))):
                            made = pe.matmul(dst, a[x][ra], b[y][rb], start=first and j == 0, stop=last and j == 2)
                        return made

                    def wait_banks(n, s, batch):
                        for name, i in s["free"].items():
                            pe.wait_ge(free_event[name], at(name, batch if name == "xt_low_done" else n, i))

                    def run(n, steps, batch=None):
                        for s in steps:
                            kind = s["kind"]
                            if "bank" in s:
                                slot = slot_of(s)
                                wait_banks(n, s, batch)
                            if kind == "x":
                                if s["c"] == 0:
                                    pe.wait_ge(x_staged, batch * 16 + 16)
                                for t in range(TB):
                                    made = pe.transpose(slot[:, t * P:(t + 1) * P],
                                                        x_stage[:, t, s["c"] * P:(s["c"] + 1) * P], ident[:])
                                made.then_inc(xt_full, 1)
                            elif kind in "qk":
                                h, half = s["head"] % 2, s["part"]
                                if kind == "q" and half == 0:
                                    pe.wait_ge(wqk_ready[h], at(f"wqk{h}_ready", n, s["head"] // 2))
                                    if batch is not None and h == 0:
                                        pe.wait_ge(xt_low_done, at("xt_low_done", batch, DC))
                                for c in range(DC):
                                    made = three(slot, wqk[h], xT, (slice(None), "qk".index(kind), c),
                                                 (slice(None), c, slice(half * BANK, (half + 1) * BANK)),
                                                 c == 0, c == DC - 1)
                                made.then_inc(slot_full, 1)
                            elif kind == "v":
                                if s["part"] == 0:
                                    pe.wait_ge(wv_ready, at("wv_ready", n, 0))
                                for t in range(2):
                                    tb = 2 * s["part"] + t
                                    for c in range(DC):
                                        made = three(slot[:, t * 2 * HD:(t + 1) * 2 * HD], xT, wv,
                                                     (slice(None), c, slice(tb * P, (tb + 1) * P)), (slice(None), c),
                                                     c == 0, c == DC - 1)
                                made.then_inc(slot_full, 1)
                            elif kind == "o":
                                if s["j"] == 0:
                                    pe.wait_ge(wo_ready, at("wo_ready", n, 0))
                                if s["part"] == 0:
                                    pe.wait_ge(unit_low_done, at("unit_low_done", n, s["j"] // 2))
                                for t in range(2):
                                    tb = 2 * s["j"] + t
                                    for h in range(2):
                                        made = three(slot[:, t * D:(t + 1) * D], headT, wo,
                                                     (slice(None), h, slice(tb * P, (tb + 1) * P)), (slice(None), h),
                                                     h == 0, h == 1)
                                made.then_inc(slot_full, 1)
                            elif kind == "score":
                                h, qi = s["head"], 4 * s["quad"] + s["i"]
                                if s["i"] == 0:
                                    done = nth_proj("k", 1, s["quad"]) if h else nth_proj("k", 2, s["quad"]) - PROJ
                                    pe.wait_ge(proj_low_done, at("proj_low_done", n, done))
                                keys = (qi + 1) * P
                                spans = [(0, min(BANK, max(keys, 2 * P)))]
                                if keys > BANK:
                                    spans.append((BANK, BANK + max(keys - BANK, 2 * P)))
                                for j, (x, y) in enumerate(((0, 0), (0, 1), (1, 0))):
                                    for lo, hi in spans:
                                        made = pe.matmul(slot[:, lo:hi], qT[h][x][:, qi * P:(qi + 1) * P],
                                                         kT[h][y][:, lo:hi], start=j == 0, stop=j == 2)
                                made.then_inc(slot_full, 1)
                            elif kind == "turn":
                                g, kb = s["quad"], s["kb"]
                                if kb == 0:
                                    pe.wait_ge(divided, at("divided", n, s["row"]))
                                for i in range(first_column(s) // P, 4):
                                    made = pe.transpose(turnP[buffer_of(s)][:, i * P:(i + 1) * P],
                                                        probs[g][:, i, kb * P:(kb + 1) * P], ident[:])
                                made.then_inc(turned, 1)
                            elif kind == "pv":
                                kb, h, lo = s["kb"], s["head"], first_column(s)
                                if kb == 0:
                                    pe.wait_ge(unit_low_done, at("unit_low_done", n, s["unit"]))
                                    if s["unit"] in (1, 2):
                                        pe.wait_ge(proj_low_done, at("proj_low_done", n, nth_proj("v", 0, 2 * s["unit"] - 1)))
                                pe.wait_ge(turn_low_done, at("turn_low_done", n, s["turn"] + 1))
                                made = three(unitP[:, lo:], v, probsT[buffer_of(s)],
                                             (slice(None), kb, slice(h * HD, (h + 1) * HD)), (slice(None), slice(lo, 4 * P)),
                                             kb == 0, s["last"])
                                made.then_inc(pv_done, 1)

                    run(0, BEFORE, 0)
                    pe.wait_ge(proj_low_done, at("proj_low_done", 0, 0))
                    with pe.Fori(0, B) as b:
                        with pe.Fori(0, PAIRS - 1) as g:
                            run(b * PAIRS + g, STEPS)
                        run(b * PAIRS + PAIRS - 1, LAST_STEPS, b + 1)
                    run(B * PAIRS, TAIL)

                @block.scalar
                def _(act):
                    def run(n, steps, batch=None):
                        for kind, s in scalar_order(steps):
                            slot = slot_of(s) if "bank" in s else None
                            if kind == "x":
                                act.wait_ge(xt_full, at("xt_full", batch, s["c"] + 1))
                                act.activation(xT[0][:, s["c"], :], slot, ACT.Copy).then_inc(xt_high, 1)
                            elif kind in "qk":
                                dst = (qT if kind == "q" else kT)[s["head"] % 2][0]
                                wait_alone(act, passed, slot_full, at("slot_full", n, s["full"] + 1))
                                act.activation(dst[:, s["part"] * BANK:(s["part"] + 1) * BANK], slot, ACT.Identity,
                                               bias=bias_cols[:, "qk".index(kind), head_at(n, s["head"])]
                                               ).then_inc(proj_high, 1)
                            elif kind == "v":
                                r = slice(2 * s["part"], 2 * s["part"] + 2)
                                act.wait_ge(slot_full, at("slot_full", n, s["full"] + 1))
                                act.activation(v[0][:, r, :], slot.rearrange("p (t n) -> p t n", t=2), ACT.Copy
                                               ).then_inc(proj_high, 1)
                            elif kind == "score":
                                quad, i, row = s["quad"], s["i"], s["row"]
                                keys = (4 * quad + i + 1) * P
                                act.wait_ge(shift_ready, at("shift_ready", n, row + 1))
                                act.activation(probs[quad][:, i, 0:keys], slot[:, 0:keys], ACT.Exp,
                                               bias=shift[:, row:row + 1], scale=SCALE,
                                               accum_out=row_sum[:, row:row + 1]).then_inc(exp_done, 1)
                            elif kind == "turn":
                                lo = first_column(s)
                                act.wait_ge(turned, at("turned", n, s["turn"] + 1))
                                act.activation(probsT[buffer_of(s)][0][:, lo:], turnP[buffer_of(s)][:, lo:],
                                               ACT.Copy).then_inc(turn_high, 1)
                            elif kind == "unit_end":
                                h, quad = s["head"], s["quad"]
                                wait_alone(act, passed, pv_done, at("pv_done", n, s["turn"] + 1))
                                act.activation(headT[0][:, h, quad * BANK:(quad + 1) * BANK], unitP[:],
                                               ACT.Identity, bias=bias_cols[:, 2, head_at(n, h - 2 if s["unit"] == 0 else h)]
                                               ).then_inc(unit_high, 1)

                    run(0, BEFORE, 0)
                    with act.Fori(0, B) as b:
                        with act.Fori(0, PAIRS - 1) as g:
                            run(b * PAIRS + g, STEPS)
                        run(b * PAIRS + PAIRS - 1, LAST_STEPS, b + 1)
                    run(B * PAIRS, TAIL)

                @block.vector
                def _(dve):
                    def run(n, steps, batch=None):
                        for kind, s in vector_order(steps):
                            slot = slot_of(s) if "bank" in s else None
                            if kind == "x":
                                c = s["c"]
                                dve.wait_ge(xt_high, at("xt_high", batch, c + 1))
                                dve.tensor_tensor(xT[1][:, c, :], slot, xT[0][:, c, :].bitcast(F32),
                                                  ALU.subtract).then_inc(xt_low_done, 1)
                            elif kind in "qk":
                                high, low = (qT if kind == "q" else kT)[s["head"] % 2]
                                r = slice(s["part"] * BANK, (s["part"] + 1) * BANK)
                                dve.wait_ge(proj_high, at("proj_high", n, s["proj"] + 1))
                                dve.scalar_tensor_tensor(low[:, r], slot, bias_cols[:, "qk".index(kind), head_at(n, s["head"])],
                                                         high[:, r].bitcast(F32), ALU.add, ALU.subtract).then_inc(proj_low_done, 1)
                            elif kind == "v":
                                r = slice(2 * s["part"], 2 * s["part"] + 2)
                                dve.wait_ge(proj_high, at("proj_high", n, s["proj"] + 1))
                                dve.tensor_tensor(v[1][:, r, :], slot.rearrange("p (t n) -> p t n", t=2),
                                                  v[0][:, r, :].bitcast(F32), ALU.subtract).then_inc(proj_low_done, 1)
                            elif kind == "o":
                                dst = stream[:, bass.ds(stream_block(n) + 2 * s["j"], 2), :]
                                dve.wait_ge(slot_full, at("slot_full", n, s["full"] + 1))
                                dve.tensor_tensor(dst, slot.rearrange("p (t n) -> p t n", t=2), dst,
                                                  ALU.add).then_inc(output_added, 1)
                            elif kind == "score":
                                qi, row = 4 * s["quad"] + s["i"], s["row"]
                                diagonal = slot[:, qi * P:(qi + 1) * P]
                                wait_alone(dve, passed, slot_full, at("slot_full", n, s["full"] + 1))
                                made = dve.tensor_tensor_reduce(diagonal, diagonal, maskneg[:], 1.0, -3e38, ALU.add, ALU.max,
                                                                row_max[:, 0, row:row + 1])
                                if qi:
                                    made = dve.reduce_max(row_max[:, 1, row:row + 1], slot[:, 0:qi * P], AX.X)
                                made.then_inc(part_max, 1)
                                dve.wait_ge(part_max, at("part_max", n, row + 1))
                                dve.tensor_scalar(shift[:, row:row + 1], row_max[:, 0, row:row + 1],
                                                  row_max[:, 1, row:row + 1] if qi else -3e38, -SCALE,
                                                  ALU.max, ALU.mult).then_inc(shift_ready, 1)
                            elif kind == "inverse":
                                row = s["row"]
                                dve.wait_ge(exp_done, at("exp_done", n, row + 1))
                                dve.reciprocal(inverse[:, row:row + 1], row_sum[:, row:row + 1]).then_inc(inverse_ready, 1)
                            elif kind == "turn":
                                lo, (high, low) = first_column(s), probsT[buffer_of(s)]
                                dve.wait_ge(turn_high, at("turn_high", n, s["turn"] + 1))
                                dve.tensor_tensor(low[:, lo:], turnP[buffer_of(s)][:, lo:], high[:, lo:].bitcast(F32),
                                                  ALU.subtract).then_inc(turn_low_done, 1)
                            elif kind == "unit_end":
                                h, quad = s["head"], s["quad"]
                                r = slice(quad * BANK, (quad + 1) * BANK)
                                dve.wait_ge(unit_high, at("unit_high", n, s["unit"] + 1))
                                dve.scalar_tensor_tensor(headT[1][:, h, r], unitP[:],
                                                         bias_cols[:, 2, head_at(n, h - 2 if s["unit"] == 0 else h)],
                                                         headT[0][:, h, r].bitcast(F32), ALU.add,
                                                         ALU.subtract).then_inc(unit_low_done, 1)

                    run(0, BEFORE, 0)
                    with dve.Fori(0, B) as b:
                        wait_alone(dve, passed, stream_in, b * 16 + 16)
                        with dve.Fori(0, PAIRS - 1) as g:
                            run(b * PAIRS + g, STEPS)
                        run(b * PAIRS + PAIRS - 1, LAST_STEPS, b + 1)
                    dve.wait_ge(consts_in, 16)
                    run(B * PAIRS, TAIL)

                @block.gpsimd
                def _(pool):
                    def flat(t, dims):
                        return t[:].rearrange(f"p {dims} -> p ({dims})")

                    pieces = {
                        "wqk0": ([flat(w, "m c n") for w in wqk[0]], flat(raw_wqk[0], "m c n"), wqk_ready[0]),
                        "wqk1": ([flat(w, "m c n") for w in wqk[1]], flat(raw_wqk[1], "m c n"), wqk_ready[1]),
                        "wv": ([flat(w, "c n") for w in wv], flat(raw_wv, "c n"), wv_ready),
                        "wo": ([flat(w, "h n") for w in wo], flat(raw_wo, "h n"), wo_ready),
                    }

                    def split(n, nth, piece, arrived, count):
                        parts, raw, ready = pieces[piece]
                        wait_alone(pool, passed, arrived, count)
                        pool.tensor_scalar(parts[0], raw, 1.0, 1.0, ALU.mult, ALU.mult).then_inc(w_high, 1)
                        pool.wait_ge(w_high, at("w_high", n, nth + 1))
                        pool.tensor_tensor(parts[1], raw, parts[0].bitcast(F32), ALU.subtract).then_inc(ready, 1)

                    def divide(n, head, quad):
                        for i in range(4):
                            row = 8 * head + 4 * quad + i
                            keys = (4 * quad + i + 1) * P
                            r = probs[quad][:, i, 0:keys]
                            wait_alone(pool, passed, inverse_ready, at("inverse_ready", n, row + 1))
                            pool.tensor_scalar(r, r, inverse[:, row:row + 1], 1.0, ALU.mult, ALU.mult).then_inc(divided, 1)

                    split(0, -3, "wqk0", raw_qk[0], 32)
                    split(0, -2, "wv", raw_v, 16)
                    split(0, -1, "wqk1", raw_qk[1], 32)
                    with pool.Fori(0, B * PAIRS) as n:
                        divide(n, 0, 0)
                        pool.wait_ge(slot_full, at("slot_full", n, nth_full("qk", 2) - SLOTS))
                        split(n, 0, "wqk0", raw_qk[0], n * 32 + 64)
                        divide(n, 0, 1)
                        pool.wait_ge(slot_full, at("slot_full", n, nth_full("v")))
                        split(n, 1, "wv", raw_v, n * 16 + 32)
                        divide(n, 1, 0)
                        pool.wait_ge(slot_full, at("slot_full", n, nth_full("o")))
                        split(n, 2, "wo", raw_o, n * 16 + 16)
                        divide(n, 1, 1)
                        pool.wait_ge(slot_full, at("slot_full", n, nth_full("qk", 1)))
                        split(n, 3, "wqk1", raw_qk[1], n * 32 + 64)

        feed_forward(nc, passed, stream, TB, ident, bo_rows, B, w_router, we_gate, we_up, we_down, ws_gate, ws_up, ws_down, out)


def feed_forward(nc, passed, stream, first, ident, bo_rows, B, w_router, we_gate, we_up, we_down, ws_gate, ws_up, ws_down, out):
    E, D, DE = we_gate.shape
    DS = ws_gate.shape[1]
    DC = D // P
    ROUTED = E * DE
    RC = ROUTED // P
    FT = ROUTED + DS
    CHUNKS = [(c * P, min(P, FT - c * P)) for c in range((FT + P - 1) // P)]
    NCH = len(CHUNKS)
    T = out.shape[1]
    NB = B * T // P
    TILE = 4 * P
    TILES = NB // 4
    EPS = 1e-5
    assert D == 2 * P and RC * P == ROUTED and NCH % 2 == 0 and E == 8

    with ExitStack() as st:
        def sb(name, shape, dt=F32):
            return st.enter_context(nc.sbuf_tensor(name, shape, dt))

        def sem(name):
            return st.enter_context(nc.semaphore(name))

        select = sb("select", [2 * E, ROUTED], F32R)
        sel_set, sel_low, sel_cut = sem("sel_set"), sem("sel_low"), sem("sel_cut")
        with nc.sbuf_tensor("band", [2 * E, 2, ROUTED], F32) as band, nc.Block() as block:
            @block.gpsimd
            def _(pool):
                flat = band[:].rearrange("p i f -> p (i f)")
                pool.memset(flat, 1.0).then_inc(sel_set, 1)
                pool.wait_ge(sel_set, 1)
                pool.affine_select(out=flat, in_=flat, compare_op=ALU.is_ge, fill=0.0, base=0,
                                   pattern=[[1, 2 * ROUTED]], channel_multiplier=-DE).then_inc(sel_low, 1)
                pool.wait_ge(sel_low, 1)
                pool.affine_select(out=flat, in_=flat, compare_op=ALU.is_ge, fill=0.0, base=DE - 1,
                                   pattern=[[-1, 2 * ROUTED]], channel_multiplier=DE).then_inc(sel_cut, 1)

            @block.vector
            def _(dve):
                dve.wait_ge(sel_cut, 1)
                dve.tensor_tensor(select[:], band[:, 0, :], band[:, 1, :], ALU.add)

        router = sb("router", [P, DC, E])
        raw = [sb(f"raw{i}", [P, FT if FT > 7 * D else 7 * D]) for i in range(2)]
        gate = [sb(f"gate_{p}", [P, DC, FT], F32R) for p in ("high", "low")]
        up = [sb(f"up_{p}", [P, DC, FT], F32R) for p in ("high", "low")]
        down = [sb(f"down_{p}", [P, NCH, D], F32R) for p in ("high", "low")]
        tokT = sb("tokT", [P, DC, TILE])
        tokT2 = [sb(f"tokT_{p}", [P, DC, TILE], F32R) for p in ("high", "low")]
        tok = sb("tok", [P, 4, D])
        stats = sb("stats", [P, 4, 6])
        moments = sb("moments", [P, 4, 2])
        spread = sb("spread", [P, 4])
        rstd = sb("rstd", [P, 4])
        neg_mean = sb("neg_mean", [P, 4])
        minus_half = sb("minus_half", [P, 4])
        logit = sb("logit", [P, NB, E])
        score = sb("score", [P, NB, E])
        pick = sb("pick", [P, NB, E])
        first_hot = sb("first_hot", [P, NB, E])
        rest = sb("rest", [P, NB, E])
        order = sb("order", [P, E])
        best = sb("best", [P, NB])
        total = sb("total", [P, NB])
        mix = sb("mix", [P, NB, 2 * E])
        mix_high = sb("mix_high", [P, NB, E], F32R)
        tok_mix = sb("tok_mix", [P, 4, 2 * E])
        mixT = sb("mixT", [2 * E, TILE], F32R)
        silu = [sb(f"silu{i}", [P, TILE]) for i in range(2)]
        both = [sb(f"both{i}", [P, TILE]) for i in range(2)]
        hid = [sb(f"hid{i}", [P, TILE]) for i in range(2)]
        hid2 = [[sb(f"hid{i}_{p}", [P, TILE], F32R) for p in ("high", "low")] for i in range(2)]
        summed = sb("summed", [P, 4, D])
        result = sb("result", [P, 4, D])

        guP = st.enter_context(nc.psum_tensor("guP", [P, 2, BANK], F32))
        mixP = st.enter_context(nc.psum_tensor("mixP", [P, BANK], F32))
        logitP = st.enter_context(nc.psum_tensor("logitP", [P, 4, E], F32))
        yP = st.enter_context(nc.psum_tensor("yP", [P, 4, BANK], F32))

        consts, w_in = sem("ffn_consts"), [sem(f"w_in{i}") for i in range(2)]
        w_high, w_low = sem("ffn_w_high"), sem("ffn_w_low")
        ready, chain = sem("half_ready"), sem("dve_chain")
        res_sum, stat_done, mom_done, normed = (sem(n) for n in ("res_sum", "stat_done", "mom_done", "normed"))
        spread_done, rstd_done = sem("spread_done"), sem("rstd_done")
        turned1, tokT_done, logits_full, logits_kept = (sem(n) for n in ("turned1", "tokT_done", "logits_full", "logits_kept"))
        exp_in, exp_out, mixed = sem("exp_in"), sem("exp_out"), sem("mixed")

        def pieces():
            for w, c in ((gate, 0), (gate, 1), (up, 0), (up, 1)):
                yield [(w, slice(0, P), (slice(None), c), 0, FT)]
            yield [(down, slice(0, P), (slice(None), slice(0, 7)), 0, 7 * D)]
            full = NCH - 8
            yield [(down, slice(0, P), (slice(None), slice(7, NCH - 1)), 0, full * D),
                   (down, slice(0, CHUNKS[-1][1]), (slice(None), NCH - 1), full * D, (full + 1) * D)]

        PIECES = list(pieces())
        LOADS = [2, 2, 2, 2, 1, 3]

        def piece_view(parts, part, rows, where):
            v = parts[part][(rows,) + tuple(where[1:])]
            return v

        def raw_view(i, rows, where, lo, hi):
            v = raw[i % 2][rows, lo:hi]
            if isinstance(where[1], slice):
                v = v.rearrange("p (c d) -> p c d", d=D)
            return v

        with nc.Block() as block:
            @block.sync
            def _(sp):
                sp.dma_start(router[:], w_router.rearrange("(c p) e -> p c e", p=P)).then_inc(consts, 16)
                for i in range(len(PIECES)):
                    if i >= 2:
                        sp.wait_ge(w_low, sum(len(x) for x in PIECES[:i - 1]))
                    s, buf = w_in[i % 2], raw[i % 2]
                    if i < 4:
                        routed, shared = ((we_gate, ws_gate), (we_up, ws_up))[i // 2]
                        r = slice((i % 2) * P, (i % 2 + 1) * P)
                        sp.dma_start(buf[:, 0:ROUTED].rearrange("p (e f) -> p e f", e=E),
                                     routed[:, r, :].rearrange("e p f -> p e f")).then_inc(s, 16)
                        sp.dma_start(buf[:, ROUTED:FT], shared[r, :]).then_inc(s, 16)
                    else:
                        flat = we_down.rearrange("e f d -> (e f) d")
                        if i == 4:
                            sp.dma_start(buf[:, 0:7 * D].rearrange("p (c d) -> p c d", d=D),
                                         flat[0:7 * P].rearrange("(c p) d -> p c d", p=P)).then_inc(s, 16)
                        else:
                            nr, ns = RC - 7, DS // P
                            sp.dma_start(buf[:, 0:nr * D].rearrange("p (c d) -> p c d", d=D),
                                         flat[7 * P:ROUTED].rearrange("(c p) d -> p c d", p=P)).then_inc(s, 16)
                            sp.dma_start(buf[:, nr * D:(nr + ns) * D].rearrange("p (c d) -> p c d", d=D),
                                         ws_down[0:ns * P].rearrange("(c p) d -> p c d", p=P)).then_inc(s, 16)
                            sp.dma_start(buf[0:DS - ns * P, (nr + ns) * D:(nr + ns + 1) * D],
                                         ws_down[ns * P:DS]).then_inc(s, 16)

            @block.gpsimd
            def _(pool):
                pool.memset(minus_half[:], -0.5).then_inc(ready, 1)
                for e in range(E):
                    made = pool.memset(order[:, e:e + 1], float(E - e))
                made.then_inc(ready, 1)
                pool.wait_ge(ready, 1)
                for j in range(TILES):
                    pool.wait_ge(mom_done, j + 1)
                    pool.tensor_scalar(spread[:], moments[:, :, 1], EPS, 1.0, ALU.add, ALU.mult).then_inc(spread_done, 1)
                    pool.wait_ge(spread_done, j + 1)
                    pool.tensor_tensor(rstd[:], spread[:], minus_half[:], ALU.pow).then_inc(rstd_done, 1)

            @block.vector
            def _(dve):
                made_low = 0
                for j in range(TILES + 1):
                    if j < TILES:
                        x = stream[:, first + 4 * j:first + 4 * j + 4, :]
                        dve.tensor_tensor(x, x, bo_rows[:].unsqueeze(1).to_broadcast([P, 4, D]), ALU.add).then_inc(res_sum, 1)
                        dve.wait_ge(res_sum, j + 1)
                        for t in range(4):
                            made = dve.bn_stats(stats[:, t, :], x[:, t, :])
                        made.then_inc(stat_done, 1)
                        dve.wait_ge(stat_done, j + 1)
                        for t in range(4):
                            made = dve.bn_aggr(moments[:, t, :], stats[:, t, :])
                        made.then_inc(mom_done, 1)
                    if 1 <= j <= len(PIECES):
                        for parts, rows, where, lo, hi in PIECES[j - 1]:
                            made_low += 1
                            dve.wait_ge(w_high, made_low)
                            dve.tensor_tensor(piece_view(parts, 1, rows, where), raw_view(j - 1, rows, where, lo, hi),
                                              piece_view(parts, 0, rows, where).bitcast(F32), ALU.subtract).then_inc(w_low, 1)
                    if j < TILES:
                        dve.wait_ge(rstd_done, j + 1)
                        for t in range(4):
                            made = dve.tensor_scalar(x[:, t, :], x[:, t, :], moments[:, t, 0:1], rstd[:, t:t + 1],
                                                     ALU.subtract, ALU.mult)
                        made.then_inc(normed, 1)

                n = [0]

                def link(made):
                    n[0] += 1
                    made.then_inc(chain, 1)
                    dve.wait_ge(chain, n[0])

                def over_experts(a):
                    return a[:].unsqueeze(2).to_broadcast([P, NB, E])

                def first_of_equal(dst, values, largest):
                    link(dve.tensor_tensor(dst[:], values[:], over_experts(largest), ALU.is_equal))
                    link(dve.tensor_tensor(dst[:], dst[:], order[:].unsqueeze(1).to_broadcast([P, NB, E]), ALU.mult))
                    link(dve.reduce_max(largest[:], dst[:], AX.X))
                    link(dve.tensor_tensor(dst[:], dst[:], over_experts(largest), ALU.is_equal))

                dve.wait_ge(logits_kept, TILES)
                dve.wait_ge(ready, 2)
                link(dve.reduce_max(best[:], logit[:], AX.X))
                dve.tensor_tensor(score[:], logit[:], over_experts(best), ALU.subtract).then_inc(exp_in, 1)
                dve.wait_ge(exp_out, 1)
                link(dve.reduce_sum(total[:], score[:], AX.X))
                link(dve.reciprocal(total[:], total[:]))
                link(dve.tensor_tensor(score[:], score[:], over_experts(total), ALU.mult))
                link(dve.reduce_max(best[:], score[:], AX.X))
                first_of_equal(first_hot, score, best)
                link(dve.scalar_tensor_tensor(rest[:], first_hot[:], -4.0, score[:], ALU.mult, ALU.add))
                link(dve.reduce_max(best[:], rest[:], AX.X))
                first_of_equal(pick, rest, best)
                link(dve.tensor_tensor(pick[:], pick[:], first_hot[:], ALU.add))
                link(dve.tensor_tensor(score[:], score[:], pick[:], ALU.mult))
                link(dve.tensor_copy(mix_high[:], score[:]))
                link(dve.tensor_copy(mix[:, :, 0:E], mix_high[:].bitcast(F32)))
                link(dve.tensor_tensor(mix[:, :, E:2 * E], score[:], mix_high[:].bitcast(F32), ALU.subtract))

            @block.tensor
            def _(pe):
                pe.wait_ge(consts, 16)
                for j in range(TILES):
                    pe.wait_ge(normed, j + 1)
                    if j:
                        pe.wait_ge(tokT_done, j)
                    for c in range(DC):
                        for t in range(4):
                            made = pe.transpose(guP[:, c, t * P:(t + 1) * P],
                                                stream[:, first + 4 * j + t, c * P:(c + 1) * P], ident[:])
                    made.then_inc(turned1, 1)
                    pe.wait_ge(tokT_done, j + 1)
                    if j:
                        pe.wait_ge(logits_kept, j)
                    for t in range(4):
                        for c in range(DC):
                            made = pe.matmul(logitP[:, t, :], tokT[:, c, t * P:(t + 1) * P], router[:, c, :],
                                             start=c == 0, stop=c == DC - 1)
                    made.then_inc(logits_full, 1)

            @block.scalar
            def _(act):
                def high(i):
                    act.wait_ge(w_in[i % 2], 16 * sum(LOADS[k] for k in range(i % 2, i + 1, 2)))
                    for parts, rows, where, lo, hi in PIECES[i]:
                        act.activation(piece_view(parts, 0, rows, where), raw_view(i, rows, where, lo, hi),
                                       ACT.Copy).then_inc(w_high, 1)

                for j in range(TILES):
                    if j < len(PIECES):
                        high(j)
                    act.wait_ge(turned1, j + 1)
                    act.activation(tokT[:], guP[:], ACT.Copy).then_inc(tokT_done, 1)
                    act.wait_ge(logits_full, j + 1)
                    act.activation(logit[:, 4 * j:4 * j + 4, :], logitP[:], ACT.Copy).then_inc(logits_kept, 1)
                act.wait_ge(exp_in, 1)
                act.activation(score[:], score[:], ACT.Exp).then_inc(exp_out, 1)

        counts = {}

        def counted(name, n):
            counts[name] = (sem(name), n)
            return counts[name][0]

        def at(name, j, i):
            return j * counts[name][1] + counts[name][1] + i

        tok_staged = counted("tok_staged", 1)
        tok_turned = counted("tok_turned", 1)
        tok_high = counted("tok_high", 1)
        tok_low = counted("tok_low", 1)
        gate_full = counted("gate_full", NCH)
        up_full = counted("up_full", NCH)
        silu_done = counted("silu_done", NCH)
        both_done = counted("both_done", RC)
        hid_done = counted("hid_done", NCH)
        hid_high = counted("hid_high", NCH)
        hid_low = counted("hid_low", NCH)
        down_full = counted("down_full", 1)
        y_added = counted("y_added", 1)
        stats2 = counted("stats2", 1)
        moments2 = counted("moments2", 1)
        spread2 = counted("spread2", 2)
        rstd2 = counted("rstd2", 1)
        result_done = counted("result_done", 1)
        stored = counted("stored", 16)

        with nc.Block() as block:
            @block.gpsimd
            def _(pool):
                for s, n in counts.values():
                    pool.sem_inc(s, n)

        with nc.Block() as block:
            @block.sync
            def _(sp):
                flat = out.rearrange("b (t p) d -> p (b t) d", p=P)
                with sp.Fori(0, TILES) as j:
                    sp.wait_ge(result_done, at("result_done", j, 1))
                    sp.dma_start(flat[:, bass.ds(j * 4, 4), :], result[:]).then_inc(stored, 16)
                sp.wait_ge(stored, 16 * (TILES + 1))

            @block.tensor
            def _(pe):
                def hidden(dst, w, c):
                    lo, m = CHUNKS[c]
                    for k in range(DC):
                        for i, (x, y) in enumerate(((1, 0), (0, 0), (0, 1))):
                            made = pe.matmul(dst[0:m], w[x][:, k, lo:lo + m], tokT2[y][:, k, :],
                                             start=k == 0 and i == 0, stop=k == DC - 1 and i == 2)
                    return made

                def project_down(j, c):
                    m = CHUNKS[c][1]
                    pe.wait_ge(hid_low, at("hid_low", j, c + 1))
                    for t in range(4):
                        for i, (x, y) in enumerate(((1, 0), (0, 0), (0, 1))):
                            made = pe.matmul(yP[:, t, 0:D], hid2[c % 2][x][0:m, t * P:(t + 1) * P], down[y][0:m, c, :],
                                             start=c == 0 and i == 0, stop=c == NCH - 1 and i == 2)
                    return made

                with pe.Fori(0, TILES) as j:
                    pe.wait_ge(tok_staged, at("tok_staged", j, 1))
                    pe.wait_ge(hid_done, at("hid_done", j, 0))
                    for c in range(DC):
                        for t in range(4):
                            pe.transpose(guP[:, c, t * P:(t + 1) * P], tok[:, t, c * P:(c + 1) * P], ident[:])
                    for t in range(4):
                        made = pe.transpose(mixP[0:2 * E, t * P:(t + 1) * P], tok_mix[:, t, :], ident[:])
                    made.then_inc(tok_turned, 1)
                    pe.wait_ge(tok_low, at("tok_low", j, 1))
                    for c in range(NCH):
                        if c:
                            pe.wait_ge(silu_done, at("silu_done", j, c))
                        hidden(guP[:, 0, :], gate, c).then_inc(gate_full, 1)
                        if c:
                            pe.wait_ge(hid_done, at("hid_done", j, c))
                        made = hidden(guP[:, 1, :], up, c)
                        if c < RC:
                            made = pe.matmul(mixP[:], select[:, c * P:(c + 1) * P], mixT[:], start=True, stop=True)
                        made.then_inc(up_full, 1)
                        if c == 1:
                            pe.wait_ge(y_added, at("y_added", j, 0))
                        if c:
                            project_down(j, c - 1)
                    project_down(j, NCH - 1).then_inc(down_full, 1)

            @block.scalar
            def _(act):
                with act.Fori(0, TILES) as j:
                    wait_alone(act, passed, tok_turned, at("tok_turned", j, 0))
                    act.activation(tok[:], stream[:, bass.ds(j * 4 + first, 4), :], ACT.Copy)
                    act.activation(tok_mix[:], mix[:, bass.ds(j * 4, 4), :], ACT.Copy).then_inc(tok_staged, 1)
                    act.wait_ge(tok_turned, at("tok_turned", j, 1))
                    act.activation(tokT2[0][:], guP[:], ACT.Copy).then_inc(tok_high, 1)
                    for c in range(NCH):
                        m = CHUNKS[c][1]
                        act.wait_ge(gate_full, at("gate_full", j, c + 1))
                        act.activation(silu[c % 2][0:m], guP[0:m, 0, :], ACT.Silu).then_inc(silu_done, 1)
                        act.wait_ge(hid_done, at("hid_done", j, c + 1))
                        act.activation(hid2[c % 2][0][0:m], hid[c % 2][0:m], ACT.Copy).then_inc(hid_high, 1)

            @block.vector
            def _(dve):
                with dve.Fori(0, TILES) as j:
                    dve.wait_ge(tok_high, at("tok_high", j, 1))
                    dve.tensor_tensor(tokT2[1][:], guP[:], tokT2[0][:].bitcast(F32), ALU.subtract)
                    dve.tensor_copy(mixT[:], mixP[0:2 * E, :]).then_inc(tok_low, 1)
                    for c in range(NCH):
                        m = CHUNKS[c][1]
                        dve.wait_ge(silu_done, at("silu_done", j, c + 1))
                        dve.wait_ge(up_full, at("up_full", j, c + 1))
                        if c < RC:
                            dve.tensor_tensor(both[c % 2][:], guP[:, 1, :], silu[c % 2][:], ALU.mult).then_inc(both_done, 1)
                            dve.wait_ge(both_done, at("both_done", j, c + 1))
                            dve.tensor_tensor(hid[c % 2][:], mixP[:], both[c % 2][:], ALU.mult).then_inc(hid_done, 1)
                        else:
                            dve.tensor_tensor(hid[c % 2][0:m], guP[0:m, 1, :], silu[c % 2][0:m], ALU.mult).then_inc(hid_done, 1)
                        dve.wait_ge(hid_high, at("hid_high", j, c + 1))
                        dve.tensor_tensor(hid2[c % 2][1][0:m], hid[c % 2][0:m], hid2[c % 2][0][0:m].bitcast(F32),
                                          ALU.subtract).then_inc(hid_low, 1)
                    dve.wait_ge(down_full, at("down_full", j, 1))
                    dve.wait_ge(result_done, at("result_done", j, 0))
                    dve.tensor_tensor(summed[:], yP[:, :, 0:D], stream[:, bass.ds(j * 4 + first, 4), :], ALU.add).then_inc(y_added, 1)
                    dve.wait_ge(y_added, at("y_added", j, 1))
                    for t in range(4):
                        made = dve.bn_stats(stats[:, t, :], summed[:, t, :])
                    made.then_inc(stats2, 1)
                    wait_alone(dve, passed, stats2, at("stats2", j, 1))
                    for t in range(4):
                        made = dve.bn_aggr(moments[:, t, :], stats[:, t, :])
                    made.then_inc(moments2, 1)

            @block.gpsimd
            def _(pool):
                with pool.Fori(0, TILES) as j:
                    wait_alone(pool, passed, moments2, at("moments2", j, 1))
                    pool.tensor_scalar(neg_mean[:], moments[:, :, 0], -1.0, 1.0, ALU.mult, ALU.mult).then_inc(spread2, 1)
                    pool.tensor_scalar(spread[:], moments[:, :, 1], EPS, 1.0, ALU.add, ALU.mult).then_inc(spread2, 1)
                    pool.wait_ge(spread2, at("spread2", j, 2))
                    pool.tensor_tensor(rstd[:], spread[:], minus_half[:], ALU.pow).then_inc(rstd2, 1)
                    pool.wait_ge(rstd2, at("rstd2", j, 1))
                    wait_alone(pool, passed, stored, at("stored", j, 0))
                    for t in range(4):
                        made = pool.tensor_scalar(result[:, t, :], summed[:, t, :], neg_mean[:, t:t + 1], rstd[:, t:t + 1],
                                                  ALU.add, ALU.mult)
                    made.then_inc(result_done, 1)


_INS = ["L0_attn_query", "L0_attn_w_q", "L0_attn_b_q", "L0_attn_w_k", "L0_attn_b_k", "L0_attn_w_v", "L0_attn_b_v",
        "L0_attn_w_o", "L0_attn_b_o", "L0_ffn_W_router", "L0_ffn_We_gate", "L0_ffn_We_up", "L0_ffn_We_down",
        "L0_ffn_Ws_gate", "L0_ffn_Ws_up", "L0_ffn_Ws_down"]


def kernel(**inputs):
    import numpy as _np
    import concourse.bacc as _bacc
    from concourse import mybir as _mybir
    from concourse.bass_utils import run_bass_kernel_spmd as _run

    nc = _bacc.Bacc("TRN2", target_bir_lowering=False, num_devices=1)
    arrays, args = {}, []
    for name in _INS:
        a = _np.ascontiguousarray(inputs[name])
        arrays[f"in_{name}"] = a
        args.append(nc.dram_tensor(f"in_{name}", a.shape, _mybir.dt.from_np(a.dtype), kind="ExternalInput").ap())
    shape = inputs["L0_attn_query"].shape
    res = nc.dram_tensor("out", shape, _mybir.dt.float32, kind="ExternalOutput")
    layer(nc, *args, res.ap())
    r = _run(nc, [arrays], core_ids=[0])
    return r.results[0]["out"]
```

```python
from contextlib import ExitStack

import concourse.bass as bass
from concourse import mybir

F32 = mybir.dt.float32
F32R = mybir.dt.float32r
ALU = mybir.AluOpType
ACT = mybir.ActivationFunctionType
AX = mybir.AxisListType

P = 128
BANK = 512


def wait_alone(engine, passed, signal, count):
    engine.wait_ge(signal, count)
    if not isinstance(count, int):
        engine.sem_inc(passed, 1)


TENSOR_ORDER = (
    "s t t o0a t p s s t p s t p q1a k1a p t t p t s s p t p t s p v0 v1 t s v2 p p o0b",
    "q1b p t k1b t t p v3 o1a s t p s p s p s t t t q2a p p t t s s p t p o1b p s t t s p",
    "t p k2a q2b p p k2b",
)
BANKS = 4
TURN_BUFFERS = 3
SCALAR_LAG = {"x": 0, "q": 2.0, "k": 2.0, "v": 2.0, "score": 4.0, "turn": 1.5, "unit_end": 0.5}
VECTOR_LAG = {"x": 0, "q": 3.0, "k": 3.0, "v": 3.0, "o": 2.0, "score": 1.0, "inverse": 5.0, "turn": 2.5, "unit_end": 1.5}


def first_column(s):
    return min(max(s["kb"] - 4 * s["quad"], 0), 2) * P


def is_edge(s):
    return s["kb"] == 4 * s["quad"] + 3


def attention_schedule(refresh=False, first=False):
    count = {"slot_full": 0, "proj_low_done": 0, "exp_done": 0, "turn": 0, "unit": 0, "output_added": 0}

    def take(kind):
        count[kind] += 1
        return count[kind] - 1

    scored = [(h, g, i) for h in range(2) for g in range(2) for i in range(4)]
    units = [(1, 1), (0, 0), (0, 1), (1, 0)]
    blocks = [(u, kb) for u, (_, g) in enumerate(units) for kb in range(4 * g + 4)]
    first_turn = [blocks.index((u, 0)) for u in range(4)]
    steps, products = [], 0
    for word in " ".join(TENSOR_ORDER).split():
        if word == "s":
            row = take("exp_done")
            h, g, i = scored[row]
            s = dict(kind="score", head=h, quad=g, i=i, row=row, frees=("exp_done", row + 1))
        elif word in "tp":
            nth = take("turn") if word == "t" else products
            products += word == "p"
            u, kb = blocks[nth]
            h, g = units[u]
            s = dict(kind="turn" if word == "t" else "pv", head=h, quad=g, kb=kb, turn=nth, unit=u,
                     row=4 * u, last=kb == 4 * g + 3)
        else:
            s = dict(kind=word[0], head=int(word[1]) if word[0] in "qk" else 0,
                     part=int(word[1]) if word[0] == "v" else "ab".index(word[2]))
            if word[0] == "o":
                nth = take("output_added")
                s.update(j=nth, frees=("output_added", nth + 1))
            else:
                nth = take("proj_low_done")
                s.update(proj=nth, frees=("proj_low_done", nth + 1))
        if "frees" in s:
            s["full"] = take("slot_full")
        steps.append(dict(s, place=len(steps)))
    count["unit"] = len(units)

    used = [-BANKS + i for i in range(BANKS)]
    for s in steps:
        if "frees" in s:
            size = 2 if s["kind"] == "score" and s["quad"] == 1 else 1
            s["bank"] = min(range(0, BANKS, size), key=lambda k: max(used[k:k + size]))
            s["banks"] = size
            used[s["bank"]:s["bank"] + size] = [s["full"]] * size
    if refresh:
        at = next(k for k, s in enumerate(steps) if s["kind"] == "q" and s["head"] == 2)
        steps[at:at] = [dict(kind="x", c=c, bank=2 * c, banks=2, frees=("xt_low_done", c + 1), place=at) for c in range(2)]

    if first:
        steps = [s for s in steps if s["kind"] != "o" and s.get("unit") != 0]
        for k, s in enumerate(s for s in steps if "full" in s):
            s["full"] = k + count["output_added"]

    last = {}
    for lap in range(2):
        for s in steps:
            if "frees" in s:
                mine = range(s["bank"], s["bank"] + s["banks"])
                s["free"] = {}
                for k in mine:
                    if k in last:
                        (name, nth), of_lap = last[k]
                        nth -= count.get(name, 0) * (lap - of_lap)
                        s["free"][name] = max(s["free"].get(name, nth), nth)
                    last[k] = (s["frees"], lap)
    return steps, count


def engine_order(steps, lag):
    items, part = [], 0
    for k, s in enumerate(steps):
        part += (s["kind"] == "x") != (k > 0 and steps[k - 1]["kind"] == "x")
        kinds = [s["kind"]] + ["inverse"] * (s["kind"] == "score") + ["unit_end"] * (s["kind"] == "pv" and s["last"])
        items += [((part, s["place"] + lag[kind]), kind, s) for kind in kinds if kind in lag]
    return [item[1:] for item in sorted(items, key=lambda item: item[0])]


def layer(nc, query, w_q, b_q, w_k, b_k, w_v, b_v, w_o, b_o, w_router, we_gate, we_up, we_down,
          ws_gate, ws_up, ws_down, out):
    B, T, D = query.shape
    HD = P
    H = w_q.shape[1] // HD
    PAIRS = H // 2
    DC = D // P
    TB = T // P
    E, _, DE = we_gate.shape
    FT = E * DE + ws_gate.shape[1]
    NCH = (FT + P - 1) // P
    assert (D, TB, HD) == (2 * P, 8, P) and H % 2 == 0
    SCALE = float(HD) ** -0.5
    MASKED = -1e10 / SCALE

    STEPS, COUNT = attention_schedule()
    LAST_STEPS, _ = attention_schedule(refresh=True)
    FIRST_STEPS, _ = attention_schedule(first=True)
    SLOTS, ROWS, TURNS, UNITS, PROJ, OUTS = (
        COUNT[k] for k in ("slot_full", "exp_done", "turn", "unit", "proj_low_done", "output_added"))
    TAIL = [s for s in STEPS if s["kind"] in ("turn", "pv") and s["unit"] == 0]
    TAIL += [dict(s, full=k, bank=k, banks=1, free={"exp_done": 0, "proj_low_done": 0, "output_added": 0})
             for k, s in enumerate(s for s in STEPS if s["kind"] == "o")]
    TAIL = [dict(s, place=k) for k, s in enumerate(TAIL)]
    X_STEPS = [s for s in LAST_STEPS if s["kind"] == "x"]
    HEAD = [dict(s, head=0, full=OUTS - 4 + k, proj=k - 4, bank=k, banks=1, free={})
            for k, s in enumerate(s for s in STEPS if s["head"] == 2 and s["kind"] in "qk")]
    BEFORE = [dict(s, free={}) for s in X_STEPS] + HEAD

    def nth_full(kinds, head=None, steps=STEPS):
        return 1 + max(s["full"] for s in steps if s["kind"] in kinds and head in (None, s["head"]))

    def nth_proj(kind, head, part):
        return 1 + next(s["proj"] for s in STEPS
                        if "proj" in s and (s["kind"], s["head"], s["part"]) == (kind, head, part))

    ctx = ExitStack()
    with ctx:
        def sem(name):
            return ctx.enter_context(nc.semaphore(name))

        totals = {}

        def counted(name, total):
            s = sem(name)
            totals[name] = (s, total)
            return s

        def credit(engine, *names):
            left_out = sum(s["kind"] == "turn" and s["unit"] == 0 for s in STEPS)
            more = dict(slot_full=OUTS - len(HEAD), proj_high=-len(HEAD), proj_low_done=-len(HEAD),
                        w_high=-3, wv_ready=-1, wqk0_ready=-1, wqk1_ready=-1, output_added=OUTS,
                        turned=left_out, pv_done=left_out, turn_high=left_out, turn_low_done=left_out,
                        unit_high=1, unit_low_done=1)
            for name in names:
                s, total = totals[name]
                if total + more.get(name, 0) > 0:
                    engine.sem_inc(s, total + more.get(name, 0))

        slot_full = counted("slot_full", SLOTS)
        turned = counted("turned", TURNS)
        pv_done = counted("pv_done", TURNS)
        exp_done = counted("exp_done", ROWS)
        turn_high = counted("turn_high", TURNS)
        unit_high = counted("unit_high", UNITS)
        proj_high = counted("proj_high", PROJ)
        part_max = counted("part_max", ROWS)
        shift_ready = counted("shift_ready", ROWS)
        inverse_ready = counted("inverse_ready", ROWS)
        turn_low_done = counted("turn_low_done", TURNS)
        unit_low_done = counted("unit_low_done", UNITS)
        proj_low_done = counted("proj_low_done", PROJ)
        output_added = counted("output_added", OUTS)
        divided = counted("divided", ROWS)
        w_high = counted("w_high", 4)
        wv_ready = counted("wv_ready", 1)
        wqk_ready = [counted(f"wqk{h}_ready", 1) for h in range(2)]
        wo_ready = counted("wo_ready", 1)
        raw_qk = [sem(f"raw_qk{h}") for h in range(2)]
        raw_v = sem("raw_v")
        raw_o = sem("raw_o")
        xt_full = counted("xt_full", DC)
        xt_high = counted("xt_high", DC)
        xt_low_done = counted("xt_low_done", DC)
        x_staged = sem("x_staged")
        consts_in = sem("consts_in")
        bias_in = sem("bias_in")
        bias_turned = sem("bias_turned")
        stream_in = sem("stream_in")
        passed = sem("passed")
        ident_zero = sem("ident_zero")
        ident_ready = sem("ident_ready")
        free_event = {"proj_low_done": proj_low_done, "exp_done": exp_done, "output_added": output_added,
                      "xt_low_done": xt_low_done}

        def at(name, n, i):
            return n * totals[name][1] + totals[name][1] + i

        def head_at(n, i):
            if isinstance(n, int):
                return slice((2 * n + i + H) % H, (2 * n + i + H) % H + 1)
            return bass.ds((n * 2 + (i + H)) % H, 1)

        def stream_block(n):
            return (n - 1) // PAIRS * TB

        def sb(stack, name, shape, dt=F32):
            return stack.enter_context(nc.sbuf_tensor(name, shape, dt))

        stream = sb(ctx, "stream", [P, B * TB, D])
        x_stage = sb(ctx, "x_stage", [P, TB, D])
        ident = sb(ctx, "ident", [P, P])
        bo_rows = sb(ctx, "bo_rows", [P, D])
        raw_ffn = [sb(ctx, f"raw_ffn{i}", [P, max(FT, NCH // 2 * D)]) for i in range(3)]
        raw_ffn.append(x_stage[:].rearrange("p t d -> p (t d)"))
        ffn_in = [sem(f"ffn_in{i}") for i in range(4)]
        ffn_weights = (we_gate, we_up, we_down, ws_gate, ws_up, ws_down)

        with ExitStack() as st:
            maskneg = sb(st, "maskneg", [P, P])
            bias_cols = sb(st, "bias_cols", [P, 3, H])
            bias_rows = sb(st, "bias_rows", [3 * H, HD])
            xT = [sb(st, f"xT_{p}", [P, DC, T], F32R) for p in ("high", "low")]
            raw_wqk = [sb(st, f"raw_wqk{h}", [P, 2, DC, HD]) for h in range(2)]
            raw_wv = sb(st, "raw_wv", [P, DC, 2 * HD])
            raw_wo = sb(st, "raw_wo", [P, 2, D])
            wqk = [[sb(st, f"wqk{h}_{p}", [P, 2, DC, HD], F32R) for p in ("high", "low")] for h in range(2)]
            wv = [sb(st, f"wv_{p}", [P, DC, 2 * HD], F32R) for p in ("high", "low")]
            wo = [sb(st, f"wo_{p}", [P, 2, D], F32R) for p in ("high", "low")]
            qT = [[sb(st, f"qT{h}_{p}", [P, T], F32R) for p in ("high", "low")] for h in range(2)]
            kT = [[sb(st, f"kT{h}_{p}", [P, T], F32R) for p in ("high", "low")] for h in range(2)]
            v = [sb(st, f"v_{p}", [P, TB, 2 * HD], F32R) for p in ("high", "low")]
            probs = [sb(st, f"probs{g}", [P, 4, 4 * (g + 1) * P]) for g in range(2)]
            probsT = [[sb(st, f"probsT{i}_{p}", [P, 4 * P], F32R) for p in ("high", "low")] for i in range(TURN_BUFFERS)]
            edgeT = [sb(st, f"edgeT_{p}", [P, 2 * P], F32R) for p in ("high", "low")]
            headT = [sb(st, f"headT_{p}", [P, 2, T], F32R) for p in ("high", "low")]
            row_max = sb(st, "row_max", [P, 2, ROWS])
            shift = sb(st, "shift", [P, ROWS])
            row_sum = sb(st, "row_sum", [P, ROWS])
            inverse = sb(st, "inverse", [P, ROWS])

            banks = st.enter_context(nc.psum_tensor("banks", [P, BANKS * BANK], F32))
            turnP = [st.enter_context(nc.psum_tensor(f"turnP{i}", [P, BANK], F32)) for i in range(TURN_BUFFERS)]
            unitP = st.enter_context(nc.psum_tensor("unitP", [P, BANK], F32))

            def slot_of(s):
                return banks[:, s["bank"] * BANK:(s["bank"] + s["banks"]) * BANK]

            def turned_block(s):
                bank, lo = turnP[s["turn"] % TURN_BUFFERS], first_column(s)
                if is_edge(s):
                    return bank[:, 3 * P:], [t[:, P:] for t in edgeT], edgeT
                parts = [t[:, lo:] for t in probsT[s["turn"] % TURN_BUFFERS]]
                return bank[:, lo:], parts, parts

            def first_score(qi):
                return (qi + 1) * P % (2 * P) if qi >= 4 else 0

            def load_qk(sp, head, pair):
                for m, w in enumerate((w_q, w_k)):
                    sp.dma_start(raw_wqk[head][:, m],
                                 w.rearrange("(c p) n -> p c n", p=P)[:, :, bass.ds(pair * 2 * HD + head * HD, HD)]
                                 ).then_inc(raw_qk[head], 16)

            def load_v(sp, pair):
                sp.dma_start(raw_wv[:], w_v.rearrange("(c p) n -> p c n", p=P)[:, :, bass.ds(pair * 2 * HD, 2 * HD)]
                             ).then_inc(raw_v, 16)

            def load_x(sp, b):
                sp.dma_start(x_stage[:], query[bass.ds(b, 1)].rearrange("o (t p) d -> p (o t) d", p=P)
                             ).then_inc(x_staged, 16)

            with nc.Block() as block:
                @block.sync
                def _(sp):
                    load_x(sp, 0)
                    load_qk(sp, 0, 0)
                    for m, bias in enumerate((b_q, b_k, b_v)):
                        sp.dma_start(bias_rows[m * H:(m + 1) * H, :], bias.rearrange("(h d) -> h d", d=HD)).then_inc(bias_in, 16)

                @block.tensor
                def _(pe):
                    pe.wait_ge(bias_in, 3 * 16)
                    pe.wait_ge(ident_ready, 1)
                    pe.transpose(turnP[0][:, 0:3 * H], bias_rows[:], ident[0:3 * H, 0:3 * H]).then_inc(bias_turned, 1)
                    credit(pe, "slot_full", "turned", "pv_done", "xt_full")

                @block.scalar
                def _(act):
                    act.wait_ge(bias_turned, 1)
                    act.activation(bias_cols[:].rearrange("p m h -> p (m h)"), turnP[0][:, 0:3 * H], ACT.Copy)
                    credit(act, "exp_done", "turn_high", "unit_high", "proj_high", "xt_high")

                @block.gpsimd
                def _(pool):
                    pool.memset(ident[:], 0.0).then_inc(ident_zero, 1)
                    pool.memset(maskneg[:], 0.0).then_inc(ident_zero, 1)
                    pool.wait_ge(ident_zero, 2)
                    pool.affine_select(out=ident[:], in_=ident[:], compare_op=ALU.not_equal, fill=1.0, base=0,
                                       pattern=[[-1, P]], channel_multiplier=1).then_inc(ident_ready, 1)
                    pool.affine_select(out=maskneg[:], in_=maskneg[:], compare_op=ALU.is_ge, fill=MASKED, base=0,
                                       pattern=[[-1, P]], channel_multiplier=1).then_inc(ident_ready, 1)
                    for part in range(2):
                        pool.memset(edgeT[part][:].bitcast(F32), 0.0)
                    credit(pool, "divided", "w_high", "wo_ready")

                @block.vector
                def _(dve):
                    credit(dve, "part_max", "shift_ready", "inverse_ready", "turn_low_done", "unit_low_done",
                           "proj_low_done", "output_added", "xt_low_done")

            with nc.Block() as block:
                @block.sync
                def _(sp):
                    load_v(sp, 0)
                    load_qk(sp, 1, 0)
                    sp.dma_start(bo_rows[:], b_o.rearrange("(o d) -> o d", o=1).to_broadcast([P, D])).then_inc(consts_in, 16)

                    for i in range(3):
                        load_piece(sp, i, raw_ffn[i], ffn_in[i], *ffn_weights)

                    def loads(n, pair, after):
                        sp.wait_ge(wqk_ready[0], at("wqk0_ready", n, 0))
                        load_qk(sp, 0, after)
                        sp.wait_ge(wv_ready, at("wv_ready", n, 0))
                        load_v(sp, after)
                        sp.wait_ge(wo_ready, at("wo_ready", n, 0))
                        sp.dma_start(raw_wo[:], w_o.rearrange("(g h d) n -> d (g h) n", h=2, d=HD)[:, bass.ds(pair * 2, 2), :]
                                     ).then_inc(raw_o, 16)
                        sp.wait_ge(wqk_ready[1], at("wqk1_ready", n, 0))
                        load_qk(sp, 1, after)

                    loads(0, 0, 1)
                    with sp.Fori(0, B - 1) as b:
                        sp.dma_start(stream[:, bass.ds(b * TB, TB), :],
                                     query[bass.ds(b, 1)].rearrange("o (t p) d -> p (o t) d", p=P)).then_inc(stream_in, 16)
                        sp.wait_ge(xt_full, at("xt_full", b, DC))
                        load_x(sp, b + 1)
                        with sp.Fori(1, PAIRS) as g:
                            loads(b * PAIRS + g, g, (g + 1) % PAIRS)
                        loads(b * PAIRS + PAIRS, 0, 1)
                    sp.dma_start(stream[:, (B - 1) * TB:B * TB, :], query[B - 1:B].rearrange("o (t p) d -> p (o t) d", p=P)
                                 ).then_inc(stream_in, 16)
                    sp.wait_ge(xt_full, at("xt_full", B - 1, DC))
                    load_piece(sp, 3, raw_ffn[3], ffn_in[3], *ffn_weights)
                    with sp.Fori(1, PAIRS) as g:
                        loads(g + (B - 1) * PAIRS, g, (g + 1) % PAIRS)

                @block.tensor
                def _(pe):
                    def three(dst, a, b, ra, rb, first, last):
                        for j, (x, y) in enumerate(((1, 0), (0, 0), (0, 1))):
                            made = pe.matmul(dst, a[x][ra], b[y][rb], start=first and j == 0, stop=last and j == 2)
                        return made

                    def wait_banks(n, s, batch):
                        for name, i in s["free"].items():
                            pe.wait_ge(free_event[name], at(name, batch if name == "xt_low_done" else n, i))

                    def run(n, steps, batch=None):
                        for s in steps:
                            kind = s["kind"]
                            if "bank" in s:
                                slot = slot_of(s)
                                wait_banks(n, s, batch)
                            if kind == "x":
                                if s["c"] == 0:
                                    pe.wait_ge(x_staged, batch * 16 + 16)
                                for t in range(TB):
                                    made = pe.transpose(slot[:, t * P:(t + 1) * P],
                                                        x_stage[:, t, s["c"] * P:(s["c"] + 1) * P], ident[:])
                                made.then_inc(xt_full, 1)
                            elif kind in "qk":
                                h, half = s["head"] % 2, s["part"]
                                if kind == "q" and half == 0:
                                    pe.wait_ge(wqk_ready[h], at(f"wqk{h}_ready", n, s["head"] // 2))
                                    if batch is not None and h == 0:
                                        pe.wait_ge(xt_low_done, at("xt_low_done", batch, DC))
                                for c in range(DC):
                                    made = three(slot, wqk[h], xT, (slice(None), "qk".index(kind), c),
                                                 (slice(None), c, slice(half * BANK, (half + 1) * BANK)),
                                                 c == 0, c == DC - 1)
                                made.then_inc(slot_full, 1)
                            elif kind == "v":
                                if s["part"] == 0:
                                    pe.wait_ge(wv_ready, at("wv_ready", n, 0))
                                for t in range(2):
                                    tb = 2 * s["part"] + t
                                    for c in range(DC):
                                        made = three(slot[:, t * 2 * HD:(t + 1) * 2 * HD], xT, wv,
                                                     (slice(None), c, slice(tb * P, (tb + 1) * P)), (slice(None), c),
                                                     c == 0, c == DC - 1)
                                made.then_inc(slot_full, 1)
                            elif kind == "o":
                                if s["j"] == 0:
                                    pe.wait_ge(wo_ready, at("wo_ready", n, 0))
                                if s["part"] == 0:
                                    pe.wait_ge(unit_low_done, at("unit_low_done", n, s["j"] // 2))
                                for t in range(2):
                                    tb = 2 * s["j"] + t
                                    for h in range(2):
                                        made = three(slot[:, t * D:(t + 1) * D], headT, wo,
                                                     (slice(None), h, slice(tb * P, (tb + 1) * P)), (slice(None), h),
                                                     h == 0, h == 1)
                                made.then_inc(slot_full, 1)
                            elif kind == "score":
                                h, qi = s["head"], 4 * s["quad"] + s["i"]
                                if s["i"] == 0:
                                    done = nth_proj("k", 1, s["quad"]) if h else nth_proj("k", 2, s["quad"]) - PROJ
                                    pe.wait_ge(proj_low_done, at("proj_low_done", n, done))
                                keys, at0 = max((qi + 1) * P, 2 * P), first_score(qi)
                                for j, (x, y) in enumerate(((0, 0), (0, 1), (1, 0))):
                                    for lo, hi in ((0, min(keys, BANK - at0)), (BANK - at0, keys)):
                                        if lo < hi:
                                            made = pe.matmul(slot[:, at0 + lo:at0 + hi], qT[h][x][:, qi * P:(qi + 1) * P],
                                                             kT[h][y][:, lo:hi], start=j == 0, stop=j == 2)
                                made.then_inc(slot_full, 1)
                            elif kind == "turn":
                                g, kb = s["quad"], s["kb"]
                                if kb == 0:
                                    pe.wait_ge(divided, at("divided", n, s["row"]))
                                first = 3 if is_edge(s) else first_column(s) // P
                                for i in range(first, 4):
                                    made = pe.transpose(turned_block(s)[0][:, (i - first) * P:(i - first + 1) * P],
                                                        probs[g][:, i, kb * P:(kb + 1) * P], ident[:])
                                made.then_inc(turned, 1)
                            elif kind == "pv":
                                kb, h, lo = s["kb"], s["head"], first_column(s)
                                if kb == 0:
                                    pe.wait_ge(unit_low_done, at("unit_low_done", n, s["unit"]))
                                    if s["unit"] in (1, 2):
                                        pe.wait_ge(proj_low_done, at("proj_low_done", n, nth_proj("v", 0, 2 * s["unit"] - 1)))
                                pe.wait_ge(turn_low_done, at("turn_low_done", n, s["turn"] + 1))
                                made = three(unitP[:, lo:], v, turned_block(s)[2],
                                             (slice(None), kb, slice(h * HD, (h + 1) * HD)), (slice(None), slice(0, 4 * P - lo)),
                                             kb == 0, s["last"])
                                made.then_inc(pv_done, 1)

                    run(0, BEFORE, 0)
                    pe.wait_ge(proj_low_done, at("proj_low_done", 0, 0))
                    run(0, FIRST_STEPS)
                    with pe.Fori(0, B - 1) as b:
                        with pe.Fori(1, PAIRS - 1) as g:
                            run(b * PAIRS + g, STEPS)
                        run(b * PAIRS + PAIRS - 1, LAST_STEPS, b + 1)
                        run(b * PAIRS + PAIRS, STEPS)
                    with pe.Fori(1, PAIRS) as g:
                        run(g + (B - 1) * PAIRS, STEPS)
                    run(B * PAIRS, TAIL)

                @block.scalar
                def _(act):
                    def run(n, steps, batch=None):
                        for kind, s in engine_order(steps, SCALAR_LAG):
                            slot = slot_of(s) if "bank" in s else None
                            if kind == "x":
                                act.wait_ge(xt_full, at("xt_full", batch, s["c"] + 1))
                                act.activation(xT[0][:, s["c"], :], slot, ACT.Copy).then_inc(xt_high, 1)
                            elif kind in "qk":
                                dst = (qT if kind == "q" else kT)[s["head"] % 2][0]
                                wait_alone(act, passed, slot_full, at("slot_full", n, s["full"] + 1))
                                act.activation(dst[:, s["part"] * BANK:(s["part"] + 1) * BANK], slot, ACT.Identity,
                                               bias=bias_cols[:, "qk".index(kind), head_at(n, s["head"])]
                                               ).then_inc(proj_high, 1)
                            elif kind == "v":
                                r = slice(2 * s["part"], 2 * s["part"] + 2)
                                act.wait_ge(slot_full, at("slot_full", n, s["full"] + 1))
                                act.activation(v[0][:, r, :], slot.rearrange("p (t n) -> p t n", t=2), ACT.Copy
                                               ).then_inc(proj_high, 1)
                            elif kind == "score":
                                quad, i, row = s["quad"], s["i"], s["row"]
                                keys = (4 * quad + i + 1) * P
                                act.wait_ge(shift_ready, at("shift_ready", n, row + 1))
                                at0 = first_score(4 * quad + i)
                                act.activation(probs[quad][:, i, 0:keys], slot[:, at0:at0 + keys], ACT.Exp,
                                               bias=shift[:, row:row + 1], scale=SCALE,
                                               accum_out=row_sum[:, row:row + 1]).then_inc(exp_done, 1)
                            elif kind == "turn":
                                source, (high, _), _ = turned_block(s)
                                act.wait_ge(turned, at("turned", n, s["turn"] + 1))
                                act.activation(high, source, ACT.Copy).then_inc(turn_high, 1)
                            elif kind == "unit_end":
                                h, quad = s["head"], s["quad"]
                                wait_alone(act, passed, pv_done, at("pv_done", n, s["turn"] + 1))
                                act.activation(headT[0][:, h, quad * BANK:(quad + 1) * BANK], unitP[:],
                                               ACT.Identity, bias=bias_cols[:, 2, head_at(n, h - 2 if s["unit"] == 0 else h)]
                                               ).then_inc(unit_high, 1)

                    run(0, BEFORE, 0)
                    run(0, FIRST_STEPS)
                    with act.Fori(0, B - 1) as b:
                        with act.Fori(1, PAIRS - 1) as g:
                            run(b * PAIRS + g, STEPS)
                        run(b * PAIRS + PAIRS - 1, LAST_STEPS, b + 1)
                        run(b * PAIRS + PAIRS, STEPS)
                    with act.Fori(1, PAIRS) as g:
                        run(g + (B - 1) * PAIRS, STEPS)
                    run(B * PAIRS, TAIL)

                @block.vector
                def _(dve):
                    def run(n, steps, batch=None):
                        for kind, s in engine_order(steps, VECTOR_LAG):
                            slot = slot_of(s) if "bank" in s else None
                            if kind == "x":
                                c = s["c"]
                                dve.wait_ge(xt_high, at("xt_high", batch, c + 1))
                                dve.tensor_tensor(xT[1][:, c, :], slot, xT[0][:, c, :].bitcast(F32),
                                                  ALU.subtract).then_inc(xt_low_done, 1)
                            elif kind in "qk":
                                high, low = (qT if kind == "q" else kT)[s["head"] % 2]
                                r = slice(s["part"] * BANK, (s["part"] + 1) * BANK)
                                dve.wait_ge(proj_high, at("proj_high", n, s["proj"] + 1))
                                dve.scalar_tensor_tensor(low[:, r], slot, bias_cols[:, "qk".index(kind), head_at(n, s["head"])],
                                                         high[:, r].bitcast(F32), ALU.add, ALU.subtract).then_inc(proj_low_done, 1)
                            elif kind == "v":
                                r = slice(2 * s["part"], 2 * s["part"] + 2)
                                dve.wait_ge(proj_high, at("proj_high", n, s["proj"] + 1))
                                dve.tensor_tensor(v[1][:, r, :], slot.rearrange("p (t n) -> p t n", t=2),
                                                  v[0][:, r, :].bitcast(F32), ALU.subtract).then_inc(proj_low_done, 1)
                            elif kind == "o":
                                dst = stream[:, bass.ds(stream_block(n) + 2 * s["j"], 2), :]
                                dve.wait_ge(slot_full, at("slot_full", n, s["full"] + 1))
                                dve.tensor_tensor(dst, slot.rearrange("p (t n) -> p t n", t=2), dst,
                                                  ALU.add).then_inc(output_added, 1)
                            elif kind == "score":
                                qi, row = 4 * s["quad"] + s["i"], s["row"]
                                at0 = first_score(qi)
                                diagonal = slot[:, at0 + qi * P:at0 + (qi + 1) * P]
                                wait_alone(dve, passed, slot_full, at("slot_full", n, s["full"] + 1))
                                made = dve.tensor_tensor_reduce(diagonal, diagonal, maskneg[:], 1.0, -3e38, ALU.add, ALU.max,
                                                                row_max[:, 0, row:row + 1])
                                if qi:
                                    made = dve.reduce_max(row_max[:, 1, row:row + 1], slot[:, at0:at0 + qi * P], AX.X)
                                made.then_inc(part_max, 1)
                                dve.wait_ge(part_max, at("part_max", n, row + 1))
                                dve.tensor_scalar(shift[:, row:row + 1], row_max[:, 0, row:row + 1],
                                                  row_max[:, 1, row:row + 1] if qi else -3e38, -SCALE,
                                                  ALU.max, ALU.mult).then_inc(shift_ready, 1)
                            elif kind == "inverse":
                                row = s["row"]
                                dve.wait_ge(exp_done, at("exp_done", n, row + 1))
                                dve.reciprocal(inverse[:, row:row + 1], row_sum[:, row:row + 1]).then_inc(inverse_ready, 1)
                            elif kind == "turn":
                                source, (high, low), _ = turned_block(s)
                                dve.wait_ge(turn_high, at("turn_high", n, s["turn"] + 1))
                                dve.tensor_tensor(low, source, high.bitcast(F32), ALU.subtract).then_inc(turn_low_done, 1)
                            elif kind == "unit_end":
                                h, quad = s["head"], s["quad"]
                                r = slice(quad * BANK, (quad + 1) * BANK)
                                dve.wait_ge(unit_high, at("unit_high", n, s["unit"] + 1))
                                dve.scalar_tensor_tensor(headT[1][:, h, r], unitP[:],
                                                         bias_cols[:, 2, head_at(n, h - 2 if s["unit"] == 0 else h)],
                                                         headT[0][:, h, r].bitcast(F32), ALU.add,
                                                         ALU.subtract).then_inc(unit_low_done, 1)

                    run(0, BEFORE, 0)
                    run(0, FIRST_STEPS)
                    with dve.Fori(0, B - 1) as b:
                        wait_alone(dve, passed, stream_in, b * 16 + 16)
                        with dve.Fori(1, PAIRS - 1) as g:
                            run(b * PAIRS + g, STEPS)
                        run(b * PAIRS + PAIRS - 1, LAST_STEPS, b + 1)
                        run(b * PAIRS + PAIRS, STEPS)
                    wait_alone(dve, passed, stream_in, B * 16)
                    with dve.Fori(1, PAIRS) as g:
                        run(g + (B - 1) * PAIRS, STEPS)
                    dve.wait_ge(consts_in, 16)
                    run(B * PAIRS, TAIL)

                @block.gpsimd
                def _(pool):
                    def flat(t, dims):
                        return t[:].rearrange(f"p {dims} -> p ({dims})")

                    pieces = {
                        "wqk0": ([flat(w, "m c n") for w in wqk[0]], flat(raw_wqk[0], "m c n"), wqk_ready[0]),
                        "wqk1": ([flat(w, "m c n") for w in wqk[1]], flat(raw_wqk[1], "m c n"), wqk_ready[1]),
                        "wv": ([flat(w, "c n") for w in wv], flat(raw_wv, "c n"), wv_ready),
                        "wo": ([flat(w, "h n") for w in wo], flat(raw_wo, "h n"), wo_ready),
                    }

                    def split(n, nth, piece, arrived, count):
                        parts, raw, ready = pieces[piece]
                        wait_alone(pool, passed, arrived, count)
                        pool.tensor_scalar(parts[0], raw, 1.0, 1.0, ALU.mult, ALU.mult).then_inc(w_high, 1)
                        pool.wait_ge(w_high, at("w_high", n, nth + 1))
                        pool.tensor_tensor(parts[1], raw, parts[0].bitcast(F32), ALU.subtract).then_inc(ready, 1)

                    def divide(n, head, quad):
                        for i in range(4):
                            row = 8 * head + 4 * quad + i
                            keys = (4 * quad + i + 1) * P
                            r = probs[quad][:, i, 0:keys]
                            wait_alone(pool, passed, inverse_ready, at("inverse_ready", n, row + 1))
                            pool.tensor_scalar(r, r, inverse[:, row:row + 1], 1.0, ALU.mult, ALU.mult).then_inc(divided, 1)

                    split(0, -3, "wqk0", raw_qk[0], 32)
                    split(0, -2, "wv", raw_v, 16)
                    split(0, -1, "wqk1", raw_qk[1], 32)

                    def run(n, steps, before):
                        divide(n, 0, 0)
                        pool.wait_ge(slot_full, at("slot_full", n, before))
                        split(n, 0, "wqk0", raw_qk[0], n * 32 + 64)
                        divide(n, 0, 1)
                        pool.wait_ge(slot_full, at("slot_full", n, nth_full("v", steps=steps)))
                        split(n, 1, "wv", raw_v, n * 16 + 32)
                        divide(n, 1, 0)
                        if steps is STEPS:
                            pool.wait_ge(slot_full, at("slot_full", n, nth_full("o")))
                        split(n, 2, "wo", raw_o, n * 16 + 16)
                        divide(n, 1, 1)
                        pool.wait_ge(slot_full, at("slot_full", n, nth_full("qk", 1, steps)))
                        split(n, 3, "wqk1", raw_qk[1], n * 32 + 64)

                    assert nth_full("qk", 2) == nth_full("qk", 2, FIRST_STEPS)
                    run(0, FIRST_STEPS, OUTS)
                    with pool.Fori(1, B * PAIRS) as n:
                        run(n, STEPS, nth_full("qk", 2) - SLOTS)

        feed_forward(nc, passed, stream, ident, bo_rows, raw_ffn, ffn_in, w_router, ffn_weights, out)


def split_pieces(gate, up, down):
    FT, (_, NCH, D) = gate[0].shape[2], down[0].shape
    for w in (gate, up):
        for c in range(w[0].shape[1]):
            yield [(w, slice(0, P), c, 0, FT)]
    half, last = NCH // 2, NCH - 1
    yield [(down, slice(0, P), slice(0, half), 0, half * D)]
    yield [(down, slice(0, P), slice(half, last), 0, (last - half) * D),
           (down, slice(0, FT - last * P), last, (last - half) * D, NCH // 2 * D)]


def load_piece(sp, i, buf, signal, we_gate, we_up, we_down, ws_gate, ws_up, ws_down):
    E, D, DE = we_gate.shape
    DS = ws_gate.shape[1]
    ROUTED = E * DE
    if i < 4:
        routed, shared = ((we_gate, ws_gate), (we_up, ws_up))[i // 2]
        r = slice((i % 2) * P, (i % 2 + 1) * P)
        sp.dma_start(buf[:, 0:ROUTED].rearrange("p (e f) -> p e f", e=E),
                     routed[:, r, :].rearrange("e p f -> p e f")).then_inc(signal, 16)
        sp.dma_start(buf[:, ROUTED:ROUTED + DS], shared[r, :]).then_inc(signal, 16)
        return 2
    flat = we_down.rearrange("e f d -> (e f) d")
    half = (ROUTED + DS + P - 1) // P // 2
    if i == 4:
        sp.dma_start(buf[:, 0:half * D].rearrange("p (c d) -> p c d", d=D),
                     flat[0:half * P].rearrange("(c p) d -> p c d", p=P)).then_inc(signal, 16)
        return 1
    nr, ns = ROUTED // P - half, DS // P
    sp.dma_start(buf[:, 0:nr * D].rearrange("p (c d) -> p c d", d=D),
                 flat[half * P:ROUTED].rearrange("(c p) d -> p c d", p=P)).then_inc(signal, 16)
    count = 1
    if ns:
        sp.dma_start(buf[:, nr * D:(nr + ns) * D].rearrange("p (c d) -> p c d", d=D),
                     ws_down[0:ns * P].rearrange("(c p) d -> p c d", p=P)).then_inc(signal, 16)
        count += 1
    sp.dma_start(buf[0:DS - ns * P, (nr + ns) * D:(nr + ns + 1) * D], ws_down[ns * P:DS]).then_inc(signal, 16)
    return count + 1


def feed_forward(nc, passed, stream, ident, bo_rows, raw, w_in, w_router, weights, out):
    we_gate, we_up, we_down, ws_gate, ws_up, ws_down = weights
    E, D, DE = we_gate.shape
    DS = ws_gate.shape[1]
    DC = D // P
    ROUTED = E * DE
    RC = ROUTED // P
    FT = ROUTED + DS
    CHUNKS = [(c * P, min(P, FT - c * P)) for c in range((FT + P - 1) // P)]
    NCH = len(CHUNKS)
    TT = 4
    TILE = TT * P
    TILES = out.shape[0] * out.shape[1] // TILE
    EPS = 1e-5
    assert D == 2 * P and RC * P == ROUTED and NCH == 14 and E == 8 and TILES % 2 == 0
    SUM, STATS, NORM, TURN, LOGITS, PICK, MIX = 2, 3, 4, (5, 6), 7, (8, 9, 10, 11), 12

    with ExitStack() as st:
        def sb(name, shape, dt=F32):
            return st.enter_context(nc.sbuf_tensor(name, shape, dt))

        def sem(name):
            return st.enter_context(nc.semaphore(name))

        select = sb("select", [2 * E, ROUTED], F32R)
        router = sb("router", [P, DC, E])
        router2 = sb("router2", [P, DC, 2 * E], F32R)
        gate = [sb(f"gate_{p}", [P, DC, FT], F32R) for p in ("high", "low")]
        up = [sb(f"up_{p}", [P, DC, FT], F32R) for p in ("high", "low")]
        down = [sb(f"down_{p}", [P, NCH, D], F32R) for p in ("high", "low")]
        tok = [sb(f"tok{i}", [P, TT, D]) for i in range(2)]
        tokT = [[sb(f"tokT{i}_{p}", [P, DC, TILE], F32R) for p in ("high", "low")] for i in range(2)]
        mixT = [sb(f"mixT{i}", [2 * E, TILE], F32R) for i in range(2)]
        stats1, stats2 = (sb(f"stats{i}", [P, TT, 6]) for i in (1, 2))
        moments1, moments2 = (sb(f"moments{i}", [P, TT, 2]) for i in (1, 2))
        spread1, spread2 = (sb(f"spread{i}", [P, TT]) for i in (1, 2))
        rstd1, rstd2 = (sb(f"rstd{i}", [P, TT]) for i in (1, 2))
        neg_mean = sb("neg_mean", [P, TT])
        minus_half = sb("minus_half", [P, TT])
        score, first_hot, rest, pick = (sb(name, [P, TT, E]) for name in ("score", "first_hot", "rest", "pick"))
        order = sb("order", [P, E])
        best, total = sb("best", [P, TT]), sb("total", [P, TT])
        mix_high = sb("mix_high", [P, TT, E], F32R)
        mix = sb("mix", [P, TT, 2 * E])
        hid2 = [[sb(f"hid{i}_{p}", [P, TILE], F32R) for p in ("high", "low")] for i in range(2)]
        result = raw[2][:, 0:TT * D].rearrange("p (t d) -> p t d", d=D)
        work = sb("work", [P, 8 * TILE])
        silu, both, hid = ([work[:, (2 * k + i) * TILE:(2 * k + i + 1) * TILE] for i in range(2)] for k in range(3))
        summed = work[:, 6 * TILE:8 * TILE].rearrange("p (t d) -> p t d", d=D)
        band = work[0:2 * E, 0:2 * ROUTED]

        gateP, upP, mixP, auxP = (st.enter_context(nc.psum_tensor(f"{name}P", [P, BANK], F32))
                                  for name in ("gate", "up", "mix", "aux"))
        yP = st.enter_context(nc.psum_tensor("yP", [P, TT, BANK], F32))
        logitP = auxP[:, 0:TT * 2 * E].rearrange("p (t e) -> p t e", e=2 * E)

        counts = {}

        def counted(name, n, before=0):
            counts[name] = (sem(f"tile_{name}"), n, before)
            return counts[name][0]

        def at(name, j, i):
            return j * counts[name][1] + (counts[name][2] + i)

        CHAIN = 20
        tok_summed = counted("tok_summed", 1)
        tok_stats = counted("tok_stats", 1)
        tok_moments = counted("tok_moments", 1)
        tok_spread = counted("tok_spread", 1)
        tok_rstd = counted("tok_rstd", 1)
        normed = counted("normed", 1)
        turned = counted("turned", DC)
        tok_high = counted("tok_high", DC)
        tok_low = counted("tok_low", DC)
        logits_full = counted("logits_full", 1)
        exp_in = counted("exp_in", 1)
        exp_out = counted("exp_out", 1)
        chain = counted("chain", CHAIN)
        mixed = counted("mixed", 1)
        mix_turned = counted("mix_turned", 1)
        mix_kept = counted("mix_kept", 1)
        gate_full = counted("gate_full", NCH)
        up_full = counted("up_full", NCH)
        silu_done = counted("silu_done", NCH)
        both_done = counted("both_done", RC)
        hid_done = counted("hid_done", NCH)
        hid_high = counted("hid_high", NCH)
        hid_low = counted("hid_low", NCH)
        down_full = counted("down_full", 1)
        y_added = counted("y_added", 1)
        y_stats = counted("y_stats", 1)
        y_moments = counted("y_moments", 1)
        y_spread = counted("y_spread", 2)
        y_rstd = counted("y_rstd", 1)
        result_done = counted("result_done", 1, 1)
        stored = counted("stored", 16, 16)

        consts = sem("ffn_consts")
        w_high, w_low = sem("ffn_w_high"), sem("ffn_w_low")
        band_set, select_done, ready, router_high = (sem(n) for n in ("band_set", "select_done", "ready", "router_high"))

        def prepare_pe_turn(pe, t, p, c, waits=True):
            if c == 0:
                pe.wait_ge(normed, at("normed", t, 1))
                if waits:
                    pe.wait_ge(mix_kept, at("mix_kept", t, 0))
            else:
                pe.wait_ge(tok_low, at("tok_low", t, c))
            for b in range(TT):
                made = pe.transpose(auxP[:, b * P:(b + 1) * P], tok[p][:, b, c * P:(c + 1) * P], ident[:])
            made.then_inc(turned, 1)

        def prepare_pe_logits(pe, t, p):
            pe.wait_ge(tok_low, at("tok_low", t, DC))
            for b in range(TT):
                for c in range(DC):
                    for x in range(2):
                        made = pe.matmul(logitP[:, b, :], tokT[p][x][:, c, b * P:(b + 1) * P], router2[:, c, :],
                                         start=c == 0 and x == 0, stop=c == DC - 1 and x == 1)
            made.then_inc(logits_full, 1)

        def prepare_pe_mix(pe, t):
            pe.wait_ge(mixed, at("mixed", t, 1))
            for b in range(TT):
                made = pe.transpose(auxP[0:2 * E, b * P:(b + 1) * P], mix[:, b, :], ident[:])
            made.then_inc(mix_turned, 1)

        def prepare_act_high(act, t, p, c):
            act.wait_ge(turned, at("turned", t, c + 1))
            act.activation(tokT[p][0][:, c, :], auxP[:], ACT.Copy).then_inc(tok_high, 1)

        def prepare_act_exp(act, t):
            wait_alone(act, passed, exp_in, at("exp_in", t, 1))
            act.activation(score[:], score[:], ACT.Exp).then_inc(exp_out, 1)

        def prepare_dve_sum(dve, t, p):
            dve.tensor_tensor(tok[p][:], stream[:, bass.ds(t * TT, TT), :],
                              bo_rows[:].unsqueeze(1).to_broadcast([P, TT, D]), ALU.add).then_inc(tok_summed, 1)

        def prepare_dve_moments(dve, t, p):
            wait_alone(dve, passed, tok_summed, at("tok_summed", t, 1))
            for b in range(TT):
                made = dve.bn_stats(stats1[:, b, :], tok[p][:, b, :])
            made.then_inc(tok_stats, 1)
            wait_alone(dve, passed, tok_stats, at("tok_stats", t, 1))
            for b in range(TT):
                made = dve.bn_aggr(moments1[:, b, :], stats1[:, b, :])
            made.then_inc(tok_moments, 1)

        def prepare_dve_norm(dve, t, p):
            wait_alone(dve, passed, tok_rstd, at("tok_rstd", t, 1))
            for b in range(TT):
                made = dve.tensor_scalar(tok[p][:, b, :], tok[p][:, b, :], moments1[:, b, 0:1], rstd1[:, b:b + 1],
                                         ALU.subtract, ALU.mult)
            made.then_inc(normed, 1)

        def prepare_dve_low(dve, t, p, c):
            dve.wait_ge(tok_high, at("tok_high", t, c + 1))
            dve.tensor_tensor(tokT[p][1][:, c, :], auxP[:], tokT[p][0][:, c, :].bitcast(F32),
                              ALU.subtract).then_inc(tok_low, 1)

        def prepare_dve_pick(dve, t, part):
            def link(k, made):
                made.then_inc(chain, 1)
                wait_alone(dve, passed, chain, at("chain", t, k))

            def over_experts(a):
                return a[:].unsqueeze(2).to_broadcast([P, TT, E])

            def first_of_equal(k, dst, values):
                link(k, dve.tensor_tensor(dst[:], values[:], over_experts(best), ALU.is_equal))
                link(k + 1, dve.tensor_tensor(dst[:], dst[:], order[:].unsqueeze(1).to_broadcast([P, TT, E]), ALU.mult))
                link(k + 2, dve.reduce_max(best[:], dst[:], AX.X))
                link(k + 3, dve.tensor_tensor(dst[:], dst[:], over_experts(best), ALU.is_equal))

            if part == 0:
                wait_alone(dve, passed, logits_full, at("logits_full", t, 1))
                link(1, dve.tensor_copy(rest[:], logitP[:, :, E:2 * E]))
                link(2, dve.tensor_tensor(score[:], logitP[:, :, 0:E], rest[:], ALU.add))
                link(3, dve.reduce_max(best[:], score[:], AX.X))
                dve.tensor_tensor(score[:], score[:], over_experts(best), ALU.subtract).then_inc(exp_in, 1)
            if part == 1:
                wait_alone(dve, passed, exp_out, at("exp_out", t, 1))
                link(4, dve.reduce_sum(total[:], score[:], AX.X))
                link(5, dve.reciprocal(total[:], total[:]))
                link(6, dve.tensor_tensor(score[:], score[:], over_experts(total), ALU.mult))
            if part == 2:
                link(7, dve.reduce_max(best[:], score[:], AX.X))
                first_of_equal(8, first_hot, score)
            if part == 3:
                link(12, dve.scalar_tensor_tensor(rest[:], first_hot[:], -4.0, score[:], ALU.mult, ALU.add))
                link(13, dve.reduce_max(best[:], rest[:], AX.X))
                first_of_equal(14, pick, rest)
            if part == 4:
                link(18, dve.tensor_tensor(pick[:], pick[:], first_hot[:], ALU.add))
                link(19, dve.tensor_tensor(score[:], score[:], pick[:], ALU.mult))
                link(20, dve.tensor_copy(mix_high[:], score[:]))
                dve.tensor_copy(mix[:, :, 0:E], mix_high[:].bitcast(F32))
                dve.tensor_tensor(mix[:, :, E:2 * E], score[:], mix_high[:].bitcast(F32), ALU.subtract).then_inc(mixed, 1)

        def prepare_dve_keep_mix(dve, t, p):
            dve.wait_ge(mix_turned, at("mix_turned", t, 1))
            dve.tensor_copy(mixT[p][:], auxP[0:2 * E, :]).then_inc(mix_kept, 1)

        def prepare_pool_rstd(pool, t):
            wait_alone(pool, passed, tok_moments, at("tok_moments", t, 1))
            pool.tensor_scalar(spread1[:], moments1[:, :, 1], EPS, 1.0, ALU.add, ALU.mult).then_inc(tok_spread, 1)
            pool.wait_ge(tok_spread, at("tok_spread", t, 1))
            pool.tensor_tensor(rstd1[:], spread1[:], minus_half[:], ALU.pow).then_inc(tok_rstd, 1)

        PIECES = list(split_pieces(gate, up, down))

        def raw_view(i, rows, cols, lo, hi):
            v = raw[i % 4][rows, lo:hi]
            return v.rearrange("p (c d) -> p c d", d=D) if isinstance(cols, slice) else v

        def tiles(engine, tile):
            tile(0, 0, True, False)
            with engine.Fori(0, (TILES - 2) // 2) as pair:
                tile(pair * 2 + 1, 1, False, False)
                tile(pair * 2 + 2, 0, False, False)
            tile(TILES - 1, 1, False, True)

        PIECES = list(split_pieces(gate, up, down))

        def raw_view(i, rows, cols, lo, hi):
            v = raw[i % 4][rows, lo:hi]
            return v.rearrange("p (c d) -> p c d", d=D) if isinstance(cols, slice) else v

        with nc.Block() as block:
            @block.sync
            def _(sp):
                sp.dma_start(router[:], w_router.rearrange("(c p) e -> p c e", p=P)).then_inc(consts, 16)
                for i in range(4, len(PIECES)):
                    sp.wait_ge(w_low, i - 3)
                    load_piece(sp, i, raw[i % 4], w_in[i % 4], *weights)
                flat = out.rearrange("b (t p) d -> p (b t) d", p=P)
                with sp.Fori(0, TILES) as j:
                    sp.wait_ge(result_done, at("result_done", j, 1))
                    sp.dma_start(flat[:, bass.ds(j * TT, TT), :], result).then_inc(stored, 16)
                sp.wait_ge(stored, at("stored", TILES, 0))

            @block.tensor
            def _(pe):
                def hidden(dst, w, c, p):
                    lo, m = CHUNKS[c]
                    for k in range(DC):
                        for i, (x, y) in enumerate(((1, 0), (0, 0), (0, 1))):
                            made = pe.matmul(dst[0:m], w[x][:, k, lo:lo + m], tokT[p][y][:, k, :],
                                             start=k == 0 and i == 0, stop=k == DC - 1 and i == 2)
                    return made

                def project_down(j, c):
                    m = CHUNKS[c][1]
                    pe.wait_ge(hid_low, at("hid_low", j, c + 1))
                    for t in range(TT):
                        for i, (x, y) in enumerate(((1, 0), (0, 0), (0, 1))):
                            made = pe.matmul(yP[:, t, 0:D], hid2[c % 2][x][0:m, t * P:(t + 1) * P], down[y][0:m, c, :],
                                             start=c == 0 and i == 0, stop=c == NCH - 1 and i == 2)
                    if c == NCH - 1:
                        made.then_inc(down_full, 1)

                PARTS_FOR = {0: 2, 1: 5, NCH // 2 + 1: 7}

                for c in range(DC):
                    prepare_pe_turn(pe, 0, 0, c, waits=False)
                prepare_pe_logits(pe, 0, 0)

                def tile(j, p, first, last):
                    for c in range(NCH):
                        if first and c in PARTS_FOR:
                            pe.wait_ge(w_low, PARTS_FOR[c])
                        if c == 0:
                            pe.wait_ge(tok_low, at("tok_low", j, DC))
                        if c or not first:
                            pe.wait_ge(silu_done, at("silu_done", j, c))
                        hidden(gateP, gate, c, p).then_inc(gate_full, 1)
                        if c or not first:
                            pe.wait_ge(hid_done, at("hid_done", j, c))
                        if first and c == 0:
                            pe.wait_ge(w_low, 4)
                        made = hidden(upP, up, c, p)
                        if c < RC:
                            if first and c == 0:
                                prepare_pe_mix(pe, 0)
                                pe.wait_ge(select_done, 1)
                            if c == 0:
                                pe.wait_ge(mix_kept, at("mix_kept", j, 1))
                            made = pe.matmul(mixP[:], select[:, c * P:(c + 1) * P], mixT[p][:], start=True, stop=True)
                        made.then_inc(up_full, 1)
                        if c == 1 and not first:
                            pe.wait_ge(y_added, at("y_added", j, 0))
                        if c:
                            project_down(j, c - 1)
                        elif not first:
                            project_down(j - 1, NCH - 1)
                        if not last:
                            if c in TURN:
                                prepare_pe_turn(pe, j + 1, 1 - p, TURN.index(c))
                            if c == LOGITS:
                                prepare_pe_logits(pe, j + 1, 1 - p)
                            if c == MIX:
                                prepare_pe_mix(pe, j + 1)
                    if last:
                        project_down(j, NCH - 1)

                tiles(pe, tile)

            @block.scalar
            def _(act):
                def high(i):
                    dmas = [2, 2, 2, 2, 1, 2 + min(1, DS // P)]
                    act.wait_ge(w_in[i % 4], 16 * sum(dmas[i % 4:i + 1:4]))
                    for parts, rows, cols, lo, hi in PIECES[i]:
                        act.activation(parts[0][rows, cols, :], raw_view(i, rows, cols, lo, hi),
                                       ACT.Copy).then_inc(w_high, 1)

                high(0)
                high(1)
                act.wait_ge(consts, 16)
                act.activation(router2[:, :, 0:E], router[:], ACT.Copy).then_inc(router_high, 1)
                high(2)
                prepare_act_high(act, 0, 0, 0)
                prepare_act_high(act, 0, 0, 1)
                high(3)
                high(4)
                prepare_act_exp(act, 0)
                high(5)
                act.wait_ge(select_done, 1)

                def tile(j, p, first, last):
                    for c in range(NCH):
                        m = CHUNKS[c][1]
                        act.wait_ge(gate_full, at("gate_full", j, c + 1))
                        act.activation(silu[c % 2][0:m], gateP[0:m], ACT.Silu).then_inc(silu_done, 1)
                        if c == LOGITS + 1 and not last:
                            prepare_act_exp(act, j + 1)
                        act.wait_ge(hid_done, at("hid_done", j, c + 1))
                        act.activation(hid2[c % 2][0][0:m], hid[c % 2][0:m], ACT.Copy).then_inc(hid_high, 1)
                        if not last:
                            if c in TURN:
                                prepare_act_high(act, j + 1, 1 - p, TURN.index(c))

                tiles(act, tile)

            @block.vector
            def _(dve):
                def low(i):
                    before = sum(len(x) for x in PIECES[:i])
                    for k, (parts, rows, cols, lo, hi) in enumerate(PIECES[i]):
                        dve.wait_ge(w_high, before + k + 1)
                        dve.tensor_tensor(parts[1][rows, cols, :], raw_view(i, rows, cols, lo, hi),
                                          parts[0][rows, cols, :].bitcast(F32), ALU.subtract).then_inc(w_low, 1)

                prepare_dve_sum(dve, 0, 0)
                prepare_dve_moments(dve, 0, 0)
                low(0)
                prepare_dve_norm(dve, 0, 0)
                dve.wait_ge(router_high, 1)
                dve.tensor_tensor(router2[:, :, E:2 * E], router[:], router2[:, :, 0:E].bitcast(F32), ALU.subtract)
                low(1)
                prepare_dve_low(dve, 0, 0, 0)
                prepare_dve_low(dve, 0, 0, 1)
                low(2)
                low(3)
                prepare_dve_pick(dve, 0, 0)
                dve.wait_ge(band_set, 1)
                for part in (1, 2, 3, 4):
                    prepare_dve_pick(dve, 0, part)
                prepare_dve_keep_mix(dve, 0, 0)
                low(4)

                def add_tokens(j, p):
                    dve.wait_ge(down_full, at("down_full", j, 1))
                    dve.wait_ge(result_done, at("result_done", j, 0))
                    dve.tensor_tensor(summed, yP[:, :, 0:D], tok[p][:], ALU.add).then_inc(y_added, 1)

                def spread_of_sum(j):
                    wait_alone(dve, passed, y_added, at("y_added", j, 1))
                    for t in range(TT):
                        made = dve.bn_stats(stats2[:, t, :], summed[:, t, :])
                    made.then_inc(y_stats, 1)
                    wait_alone(dve, passed, y_stats, at("y_stats", j, 1))
                    for t in range(TT):
                        made = dve.bn_aggr(moments2[:, t, :], stats2[:, t, :])
                    made.then_inc(y_moments, 1)

                def tile(j, p, first, last):
                    for c in range(NCH):
                        m = CHUNKS[c][1]
                        dve.wait_ge(silu_done, at("silu_done", j, c + 1))
                        dve.wait_ge(up_full, at("up_full", j, c + 1))
                        if c < RC:
                            dve.tensor_tensor(both[c % 2], upP[:], silu[c % 2], ALU.mult).then_inc(both_done, 1)
                            dve.wait_ge(both_done, at("both_done", j, c + 1))
                            dve.tensor_tensor(hid[c % 2], mixP[:], both[c % 2], ALU.mult).then_inc(hid_done, 1)
                        else:
                            dve.tensor_tensor(hid[c % 2][0:m], upP[0:m], silu[c % 2][0:m], ALU.mult).then_inc(hid_done, 1)
                        if c == 0 and not first:
                            add_tokens(j - 1, 1 - p)
                        dve.wait_ge(hid_high, at("hid_high", j, c + 1))
                        dve.tensor_tensor(hid2[c % 2][1][0:m], hid[c % 2][0:m], hid2[c % 2][0][0:m].bitcast(F32),
                                          ALU.subtract).then_inc(hid_low, 1)
                        if c == 1 and not first:
                            spread_of_sum(j - 1)
                        if first and c == 1:
                            low(5)
                        if not last:
                            if c == SUM:
                                prepare_dve_sum(dve, j + 1, 1 - p)
                            if c == STATS:
                                prepare_dve_moments(dve, j + 1, 1 - p)
                            if c == NORM:
                                prepare_dve_norm(dve, j + 1, 1 - p)
                            if c in TURN:
                                prepare_dve_low(dve, j + 1, 1 - p, TURN.index(c))
                            if c == LOGITS:
                                prepare_dve_pick(dve, j + 1, 0)
                            if c in PICK:
                                prepare_dve_pick(dve, j + 1, 1 + PICK.index(c))
                            if c == MIX:
                                prepare_dve_keep_mix(dve, j + 1, 1 - p)
                    if last:
                        add_tokens(j, p)
                        spread_of_sum(j)

                tiles(dve, tile)

            @block.gpsimd
            def _(pool):
                pool.memset(minus_half[:], -0.5)
                for e in range(E):
                    pool.memset(order[:, e:e + 1], float(E - e))
                pool.memset(band, 1.0).then_inc(band_set, 1)
                pool.wait_ge(band_set, 1)
                prepare_pool_rstd(pool, 0)
                pool.affine_select(out=band, in_=band, compare_op=ALU.is_ge, fill=0.0, base=0,
                                   pattern=[[1, 2 * ROUTED]], channel_multiplier=-DE).then_inc(band_set, 1)
                pool.wait_ge(band_set, 2)
                pool.affine_select(out=band, in_=band, compare_op=ALU.is_ge, fill=0.0, base=DE - 1,
                                   pattern=[[-1, 2 * ROUTED]], channel_multiplier=DE).then_inc(band_set, 1)
                pool.wait_ge(band_set, 3)
                pool.tensor_tensor(select[:], band[:, 0:ROUTED], band[:, ROUTED:2 * ROUTED], ALU.add).then_inc(select_done, 1)
                pool.sem_inc(result_done, 1)
                pool.sem_inc(stored, 16)

                def finish(j):
                    wait_alone(pool, passed, y_moments, at("y_moments", j, 1))
                    pool.tensor_scalar(neg_mean[:], moments2[:, :, 0], -1.0, 1.0, ALU.mult, ALU.mult).then_inc(y_spread, 1)
                    pool.tensor_scalar(spread2[:], moments2[:, :, 1], EPS, 1.0, ALU.add, ALU.mult).then_inc(y_spread, 1)
                    pool.wait_ge(y_spread, at("y_spread", j, 2))
                    pool.tensor_tensor(rstd2[:], spread2[:], minus_half[:], ALU.pow).then_inc(y_rstd, 1)
                    pool.wait_ge(y_rstd, at("y_rstd", j, 1))
                    wait_alone(pool, passed, stored, at("stored", j, 0))
                    for t in range(TT):
                        made = pool.tensor_scalar(result[:, t, :], summed[:, t, :], neg_mean[:, t:t + 1], rstd2[:, t:t + 1],
                                                  ALU.add, ALU.mult)
                    made.then_inc(result_done, 1)

                def tile(j, p, first, last):
                    if not first:
                        finish(j - 1)
                    if not last:
                        prepare_pool_rstd(pool, j + 1)
                    else:
                        finish(j)

                tiles(pool, tile)


_INS = ["L0_attn_query", "L0_attn_w_q", "L0_attn_b_q", "L0_attn_w_k", "L0_attn_b_k", "L0_attn_w_v", "L0_attn_b_v",
        "L0_attn_w_o", "L0_attn_b_o", "L0_ffn_W_router", "L0_ffn_We_gate", "L0_ffn_We_up", "L0_ffn_We_down",
        "L0_ffn_Ws_gate", "L0_ffn_Ws_up", "L0_ffn_Ws_down"]


def kernel(**inputs):
    import numpy as _np
    import concourse.bacc as _bacc
    from concourse import mybir as _mybir
    from concourse.bass_utils import run_bass_kernel_spmd as _run

    nc = _bacc.Bacc("TRN2", target_bir_lowering=False, num_devices=1)
    arrays, args = {}, []
    for name in _INS:
        a = _np.ascontiguousarray(inputs[name])
        arrays[f"in_{name}"] = a
        args.append(nc.dram_tensor(f"in_{name}", a.shape, _mybir.dt.from_np(a.dtype), kind="ExternalInput").ap())
    shape = inputs["L0_attn_query"].shape
    res = nc.dram_tensor("out", shape, _mybir.dt.float32, kind="ExternalOutput")
    layer(nc, *args, res.ap())
    r = _run(nc, [arrays], core_ids=[0])
    return r.results[0]["out"]
```
